# Optimizing a Trainium2 kernel written in Bass

```python
import numpy as np
import jax
import jax.numpy as jnp

def _softmax(x, axis=-1):
    return jax.nn.softmax(x, axis=axis)

def _gelu(x):
    return jax.nn.gelu(x, approximate=True)

def _silu(x):
    return jax.nn.silu(x)

def _sigmoid(x):
    return jax.nn.sigmoid(x)

def _layernorm(x, axis=-1, eps=1e-05):
    m = jnp.mean(x, axis=axis, keepdims=True)
    v = jnp.var(x, axis=axis, keepdims=True)
    return (x - m) / jnp.sqrt(v + eps)

def _scatter_add(tgt, idx, src, axis=0):
    return tgt.at[idx].add(src)

def _segment_sum(src, seg, n):
    return jax.ops.segment_sum(src, seg, n)
kernel_name = 'mk_adj_ffn_d2_adj_r2_50359f'

def setup_inputs(seed: int=0):
    np.random.seed(seed)
    _w = jnp.asarray

    def _rec_inputs():
        import jax
        import jax.numpy as jnp
        _gk = jax.random.key(seed)
        x = -0.0002928 + 1 * jax.random.normal(jax.random.fold_in(_gk, 1), (128, 64, 128), jnp.float32)
        _a = jax.random.bernoulli(jax.random.fold_in(_gk, 2), 0.0625, (128, 64, 64))
        adj = _a.astype(jnp.int32)
        return (x, adj)
    x, adj = _rec_inputs()

    def _L0_gnn_setup():
        import jax, jax.numpy as jnp
        import numpy as np
        NEG_INF = -1000000000.0
        LEAKY_SLOPE = 0.2
        key = jax.random.key(seed)
        k1, k2, k3, k4 = jax.random.split(key, 4)
        B, N, D_in, D_out = (8, 1024, 128, 128)
        x = jax.random.normal(k1, (B, N, D_in), dtype=jnp.float32)
        adj_matrix = jax.random.randint(k2, (B, N, N), 0, 2, dtype=jnp.int32)
        W = jax.random.normal(k3, (D_out, D_in), dtype=jnp.float32) / np.sqrt(D_in)
        a = jax.random.normal(k4, (1, 2 * D_out), dtype=jnp.float32) / np.sqrt(2 * D_out)
        return {'x': x, 'adj_matrix': adj_matrix, 'W': W, 'a': a}
    _L0_gnn_all = _L0_gnn_setup()
    _L0_gnn_in = {k: v for k, v in _L0_gnn_all.items() if k in ('W', 'a')}
    del _L0_gnn_all

    def _L0_ffn_setup():
        import jax, jax.numpy as jnp
        import numpy as np
        DIM = 128
        HEADS = 8
        NUM_KEYS = 128
        NUM_KV = NUM_KEYS ** 2
        PK_TOPK = 16
        FINAL_TOPK = 16
        DIM_KEY = DIM // 2
        P = 2

        def _pk(x, Wq_pk, pk_keys):
            b, n, _ = x.shape
            q = (x @ Wq_pk).reshape(b, n, P, HEADS, DIM_KEY).transpose(2, 0, 1, 3, 4)
            sim = jnp.einsum('pbnhd,pkhd->pbnhk', q, pk_keys)
            scores, idx = jax.lax.top_k(sim, PK_TOPK)
            idx0 = idx[0]
            idx1 = idx[1] * NUM_KEYS
            index = (idx0[..., :, None] + idx1[..., None, :]).reshape(b, n, HEADS, PK_TOPK * PK_TOPK)
            score = (scores[0][..., :, None] + scores[1][..., None, :]).reshape(b, n, HEADS, PK_TOPK * PK_TOPK)
            final_scores, pk_idx = jax.lax.top_k(score, FINAL_TOPK)
            final_indices = jnp.take_along_axis(index, pk_idx, axis=-1)
            final_scores = jax.nn.softmax(final_scores, axis=-1)
            return (final_scores, final_indices)
        key = jax.random.key(seed)
        ks = jax.random.split(key, 7)
        b, n = (2, 512)
        std = 0.02
        x = jax.random.normal(ks[0], (b, n, DIM), dtype=jnp.float32)
        Wq_pk = jax.random.normal(ks[1], (DIM, P * HEADS * DIM_KEY), dtype=jnp.float32) * std
        pk_keys = jax.random.normal(ks[2], (P, NUM_KEYS, HEADS, DIM_KEY), dtype=jnp.float32) * std
        Wq = jax.random.normal(ks[3], (DIM, HEADS * DIM), dtype=jnp.float32) * std
        keys_table = jax.random.normal(ks[4], (NUM_KV * HEADS, DIM), dtype=jnp.float32) * std
        values_table = jax.random.normal(ks[5], (NUM_KV * HEADS, DIM), dtype=jnp.float32) * std
        Wo = jax.random.normal(ks[6], (DIM * HEADS, DIM), dtype=jnp.float32) * std
        return {'x': x, 'Wq_pk': Wq_pk, 'pk_keys': pk_keys, 'Wq': Wq, 'keys_table': keys_table, 'values_table': values_table, 'Wo': Wo}
    _L0_ffn_all = _L0_ffn_setup()
    _L0_ffn_in = {k: v for k, v in _L0_ffn_all.items() if k in ('Wq_pk', 'pk_keys', 'Wq', 'keys_table', 'values_table', 'Wo')}
    del _L0_ffn_all

    def _L1_gnn_setup():
        import jax, jax.numpy as jnp
        import numpy as np
        key = jax.random.key(seed)
        k1, k2, k3, k4 = jax.random.split(key, 4)
        B, N, F, U = (8, 1024, 128, 128)
        x = jax.random.normal(k1, (B, N, F), dtype=jnp.float32)
        adj = jax.random.randint(k2, (B, N, N), 0, 2, dtype=jnp.int32)
        W_msg = jax.random.normal(k3, (F, U), dtype=jnp.float32) / np.sqrt(F)
        W_upd = jax.random.normal(k4, (F, U), dtype=jnp.float32) / np.sqrt(F)
        bias = jnp.zeros((U,), dtype=jnp.float32)
        return {'x': x, 'adj': adj, 'W_msg': W_msg, 'W_upd': W_upd, 'bias': bias}
    _L1_gnn_all = _L1_gnn_setup()
    _L1_gnn_in = {k: v for k, v in _L1_gnn_all.items() if k in ('W_msg', 'W_upd', 'bias')}
    del _L1_gnn_all

    def _L1_ffn_setup():
        import jax, jax.numpy as jnp
        import numpy as np
        B, S, D = (8, 2048, 128)
        H = 4 * D
        CAPACITY = 0.5
        key = jax.random.key(seed)
        ks = jax.random.split(key, 6)
        x = jax.random.normal(ks[0], (B, S, D), dtype=jnp.float32)
        attention_mask = jnp.zeros((B, 1, 1, S), dtype=jnp.float32)
        wr = jax.random.normal(ks[1], (D, 1), dtype=jnp.float32) * 0.02
        br = jnp.zeros((1,), dtype=jnp.float32)
        w1 = jax.random.normal(ks[2], (D, H), dtype=jnp.float32) * 0.02
        b1 = jnp.zeros((H,), dtype=jnp.float32)
        w2 = jax.random.normal(ks[3], (H, D), dtype=jnp.float32) * 0.02
        b2 = jnp.zeros((D,), dtype=jnp.float32)
        return {'x': x, 'attention_mask': attention_mask, 'wr': wr, 'br': br, 'w1': w1, 'b1': b1, 'w2': w2, 'b2': b2}
    _L1_ffn_all = _L1_ffn_setup()
    _L1_ffn_in = {k: v for k, v in _L1_ffn_all.items() if k in ('attention_mask', 'wr', 'br', 'w1', 'b1', 'w2', 'b2')}
    del _L1_ffn_all
    return {'x': x, 'adj': adj, 'L0_gnn_W': _L0_gnn_in['W'], 'L0_gnn_a': _L0_gnn_in['a'], 'L0_ffn_Wq_pk': _L0_ffn_in['Wq_pk'], 'L0_ffn_pk_keys': _L0_ffn_in['pk_keys'], 'L0_ffn_Wq': _L0_ffn_in['Wq'], 'L0_ffn_keys_table': _L0_ffn_in['keys_table'], 'L0_ffn_values_table': _L0_ffn_in['values_table'], 'L0_ffn_Wo': _L0_ffn_in['Wo'], 'L1_gnn_W_msg': _L1_gnn_in['W_msg'], 'L1_gnn_W_upd': _L1_gnn_in['W_upd'], 'L1_gnn_bias': _L1_gnn_in['bias'], 'L1_ffn_attention_mask': _L1_ffn_in['attention_mask'], 'L1_ffn_wr': _L1_ffn_in['wr'], 'L1_ffn_br': _L1_ffn_in['br'], 'L1_ffn_w1': _L1_ffn_in['w1'], 'L1_ffn_b1': _L1_ffn_in['b1'], 'L1_ffn_w2': _L1_ffn_in['w2'], 'L1_ffn_b2': _L1_ffn_in['b2']}

def reference(x, adj, L0_gnn_W, L0_gnn_a, L0_ffn_Wq_pk, L0_ffn_pk_keys, L0_ffn_Wq, L0_ffn_keys_table, L0_ffn_values_table, L0_ffn_Wo, L1_gnn_W_msg, L1_gnn_W_upd, L1_gnn_bias, L1_ffn_attention_mask, L1_ffn_wr, L1_ffn_br, L1_ffn_w1, L1_ffn_b1, L1_ffn_w2, L1_ffn_b2):
    import jax
    import jax.numpy as jnp

    def _L0_gnn_ref(x, adj_matrix, W, a):
        import jax, jax.numpy as jnp
        import numpy as np
        NEG_INF = -1000000000.0
        LEAKY_SLOPE = 0.2
        h = jnp.einsum('bnd,od->bno', x, W)
        D = h.shape[-1]
        a_left, a_right = (a[0, :D], a[0, D:])
        e = (h @ a_left)[:, :, None] + (h @ a_right)[:, None, :]
        e = jnp.where(e > 0, e, LEAKY_SLOPE * e)
        e = jnp.where(adj_matrix == 0, NEG_INF, e)
        alpha = jax.nn.softmax(e, axis=-1)
        return jnp.einsum('bij,bjd->bid', alpha, h)

    def _L0_ffn_ref(x, Wq_pk, pk_keys, Wq, keys_table, values_table, Wo):
        import jax, jax.numpy as jnp
        import numpy as np
        DIM = 128
        HEADS = 8
        NUM_KEYS = 128
        NUM_KV = NUM_KEYS ** 2
        PK_TOPK = 16
        FINAL_TOPK = 16
        DIM_KEY = DIM // 2
        P = 2

        def _pk(x, Wq_pk, pk_keys):
            b, n, _ = x.shape
            q = (x @ Wq_pk).reshape(b, n, P, HEADS, DIM_KEY).transpose(2, 0, 1, 3, 4)
            sim = jnp.einsum('pbnhd,pkhd->pbnhk', q, pk_keys)
            scores, idx = jax.lax.top_k(sim, PK_TOPK)
            idx0 = idx[0]
            idx1 = idx[1] * NUM_KEYS
            index = (idx0[..., :, None] + idx1[..., None, :]).reshape(b, n, HEADS, PK_TOPK * PK_TOPK)
            score = (scores[0][..., :, None] + scores[1][..., None, :]).reshape(b, n, HEADS, PK_TOPK * PK_TOPK)
            final_scores, pk_idx = jax.lax.top_k(score, FINAL_TOPK)
            final_indices = jnp.take_along_axis(index, pk_idx, axis=-1)
            final_scores = jax.nn.softmax(final_scores, axis=-1)
            return (final_scores, final_indices)
        b, n, d = x.shape
        q = (x @ Wq).reshape(b, n, HEADS, DIM) * DIM ** (-0.5)
        kv_scores, indices = _pk(x, Wq_pk, pk_keys)
        offsets = jnp.arange(HEADS, dtype=indices.dtype) * NUM_KV
        ind = indices + offsets[None, None, :, None]
        k = jnp.einsum('bnhk,bnhkd->bnhd', kv_scores, keys_table[ind])
        v = jnp.einsum('bnhk,bnhkd->bnhd', kv_scores, values_table[ind])
        sim = jnp.einsum('bihd,bjhd->bhij', q, k)
        neg = -jnp.finfo(sim.dtype).max
        causal = jnp.tril(jnp.ones((n, n), dtype=bool))
        sim = jnp.where(causal, sim, neg)
        attn = jax.nn.softmax(sim, axis=-1)
        out = jnp.einsum('bhij,bjhd->bhid', attn, v)
        out = out.transpose(0, 2, 1, 3).reshape(b, n, HEADS * DIM)
        return out @ Wo

    def _L1_gnn_ref(x, adj, W_msg, W_upd, bias):
        import jax, jax.numpy as jnp
        import numpy as np
        a = adj.astype(x.dtype)
        h = jnp.einsum('bnf,fu->bnu', x, W_msg)
        msg_sum = jnp.einsum('bij,biu->bju', a, h)
        deg = jnp.sum(a, axis=1)
        messages = jnp.where(deg[..., None] > 0, msg_sum / jnp.maximum(deg, 1.0)[..., None], 0.0)
        out = jnp.einsum('bnf,fu->bnu', x, W_upd) + messages + bias
        return jax.nn.relu(out)

    def _L1_ffn_ref(x, attention_mask, wr, br, w1, b1, w2, b2):
        import jax, jax.numpy as jnp
        import numpy as np
        B, S, D = (8, 2048, 128)
        H = 4 * D
        CAPACITY = 0.5
        b, s, d = x.shape
        weights = (jnp.einsum('bsd,do->bso', x, wr) + br)[..., 0]
        k = max(1, int(CAPACITY * s))
        kk = k - 1 if k > 1 else 1
        _, idx = jax.lax.top_k(weights, k)
        sel_idx = idx[:, :kk]
        sel = jnp.take_along_axis(x, sel_idx[:, :, None], axis=1)
        h = jax.nn.gelu(jnp.einsum('bkd,dh->bkh', sel, w1) + b1)
        y = jnp.einsum('bkh,hd->bkd', h, w2) + b2
        w_sel = jnp.take_along_axis(weights, sel_idx, axis=1)
        y = y * w_sel[..., None]
        batch_idx = jnp.arange(b)[:, None]
        processed = jnp.zeros_like(x).at[batch_idx, sel_idx].set(y)
        return processed + x
    x = x + _L0_gnn_ref(_layernorm(x, axis=-1), adj, L0_gnn_W, L0_gnn_a)
    x = x + _L0_ffn_ref(_layernorm(x, axis=-1), L0_ffn_Wq_pk, L0_ffn_pk_keys, L0_ffn_Wq, L0_ffn_keys_table, L0_ffn_values_table, L0_ffn_Wo)
    x = x + _L1_gnn_ref(_layernorm(x, axis=-1), adj, L1_gnn_W_msg, L1_gnn_W_upd, L1_gnn_bias)
    x = x + _L1_ffn_ref(_layernorm(x, axis=-1), L1_ffn_attention_mask, L1_ffn_wr, L1_ffn_br, L1_ffn_w1, L1_ffn_b1, L1_ffn_w2, L1_ffn_b2)
    return x

_drawn_inputs = setup_inputs


def setup_inputs(seed=0):
    import zlib

    import numpy as np

    out = dict(_drawn_inputs(seed))
    spreads = {'L1_gnn_bias': (0.0, 0.1), 'L1_ffn_b1': (0.0, 0.8), 'L1_ffn_b2': (0.0, 0.8)}
    factors = {'L0_ffn_Wq_pk': 8.0,
     'L0_ffn_pk_keys': 8.0,
     'L0_ffn_Wq': 34.087,
     'L0_ffn_keys_table': 33.645,
     'L0_ffn_values_table': 8.0,
     'L0_ffn_Wo': 8.0,
     'L1_ffn_wr': 8.0,
     'L1_ffn_w1': 8.0,
     'L1_ffn_w2': 8.0}
    for name, (base, spread) in spreads.items():
        noise = np.random.default_rng([zlib.crc32(name.encode()), seed]).standard_normal(out[name].shape)
        drawn = base * np.exp(spread * noise) if base else spread * noise
        out[name] = jnp.asarray(drawn.astype(out[name].dtype))
    for name, factor in factors.items():
        out[name] = (out[name] * factor).astype(out[name].dtype)
    return out
```

```python
from contextlib import ExitStack

import numpy as np
import concourse.bass as bass
from concourse import mybir

ALU = mybir.AluOpType
ACT = mybir.ActivationFunctionType
AX = mybir.AxisListType
F32 = mybir.dt.float32
U32 = mybir.dt.uint32
I32 = mybir.dt.int32

P = 128
G = 64
D = 128
H = 8
TOPK = 16
NKEY = 128
DK = 64
HID = 512
HC = HID // P
KEPT = 31
SLOTS = 4
EPS = 1e-5
NEG_EDGE = -1.0e9
NEG_CAUSAL = -1.0e30
NEG_TAKEN = -3.0e38
GELU_C = 1.5957691216057308
GELU_A = 0.044715

BLOCKS = ((0, 1, 16), (1, 1, 8), (2, 2, 5), (4, 4, 3), (8, 8, 1))
CAND = sum(ni * nj for _, ni, nj in BLOCKS)


class Tile:

    def __init__(self, i, p):
        self.i, self.p, self.n = i, p, i * 2 + p

    def next(self):
        return Tile(self.i, 1) if self.p == 0 else Tile(self.i + 1, 0)


class Steps:

    def __init__(self, eng, sem):
        self.eng, self.sem, self.count = eng, sem, 0

    def mark(self, ins):
        self.count += 1
        ins.then_inc(self.sem, 1)

    def settle(self):
        self.eng.wait_ge(self.sem, self.count)

    def then(self, ins):
        self.mark(ins)
        self.settle()

    def restart(self):
        self.settle()
        self.eng.sem_clear(self.sem)
        self.count = 0


def build(nc, x, adj, gat_wT, gat_a, wq_pk, keysT, wq, table, wo, w_msg, w_upd, bias, wr, br, w1, b1, w2, b2, out):
    TILES = x.shape[0] // P
    ctx = ExitStack()
    with ctx:
        def sb(name, shape, dt=F32):
            return ctx.enter_context(nc.sbuf_tensor(name, shape, dt))

        def sem(name):
            return ctx.enter_context(nc.semaphore(name))

        def sems(name, n):
            return [sem(f"{name}{i}") for i in range(n)]

        ident = sb("ident", [P, P])
        ident_g = sb("ident_g", [P, G])
        before_g = sb("before_g", [P, G])
        before = sb("before", [P, P])
        causal = sb("causal", [P, P])
        neg_edge = sb("neg_edge", [P, G])
        cand_pos_i = sb("cand_pos_i", [P, CAND], I32)
        cand_pos = sb("cand_pos", [P, CAND])
        gat_w_sb = sb("gat_w_sb", [P, D])
        a_cols = sb("a_cols", [P, 2])
        a_left = sb("a_left", [P, P])
        a_right = sb("a_right", [P, P])
        wq_pk_sb = sb("wq_pk_sb", [P, 2 * H * DK])
        keys_sb = sb("keys_sb", [P, H, 2, NKEY])
        wq_sb = sb("wq_sb", [P, H * D])
        wo_sb = sb("wo_sb", [P, H, D])
        w_msg_sb = sb("w_msg_sb", [P, D])
        w_upd_sb = sb("w_upd_sb", [P, D])
        bias_sb = sb("bias_sb", [P, D])
        wr_col = sb("wr_col", [P, 1])
        wr_sb = sb("wr_sb", [P, P])
        br_sb = sb("br_sb", [P, 1])
        w1_sb = sb("w1_sb", [P, HID])
        b1_sb = sb("b1_sb", [P, HC])
        w2_sb = sb("w2_sb", [P, HC, D])
        b2_sb = sb("b2_sb", [P, D])

        x_in = sb("x_in", [P, 2, D])
        adj_in = sb("adj_in", [P, 2, G], I32)
        adj_f = sb("adj_f", [P, 2, P])
        x1 = sb("x1", [P, 2, D])
        qT = sb("qT", [P, 2, H, P])
        row_idx = sb("row_idx", [P, 2, H, TOPK], U32)
        row_w = sb("row_w", [P, 2, H, TOPK])
        out_sb = sb("out_sb", [P, 2, D])

        ln_stats = sb("ln_stats", [P, 4, 6])
        ln_mv = sb("ln_mv", [P, 4, 2])
        ln_ve = sb("ln_ve", [P, 4])
        ln_log = sb("ln_log", [P, 4])
        ln_r0 = sb("ln_r0", [P, 4])
        ln_c = sb("ln_c", [P, 4])
        ln_r = sb("ln_r", [P, 4])
        xn = sb("xn", [P, 4, D])
        xnT = sb("xnT", [P, 4, P])

        gh_sb = sb("gh_sb", [P, D])
        ghT_sb = sb("ghT_sb", [P, P])
        no_edge = sb("no_edge", [P, G], I32)
        edge_raw = sb("edge_raw", [P, G])
        edge = sb("edge", [P, G])
        gat_negmax = sb("gat_negmax", [P, 1])
        gat_sum = sb("gat_sum", [P, 1])
        gat_rsum = sb("gat_rsum", [P, 1])
        gat_p = sb("gat_p", [P, P])
        gat_pT_sb = sb("gat_pT_sb", [P, P])

        qpT = sb("qpT", [P, H, P])
        best = sb("best", [P, 2, 2, TOPK])
        best_u = sb("best_u", [P, 2, 2, TOPK], U32)
        best_f = sb("best_f", [P, 2, 2, TOPK])
        left = sb("left", [P, 4, NKEY])
        pair_s = sb("pair_s", [P, 2, CAND])
        pair_i = sb("pair_i", [P, 2, CAND])
        pair_left = sb("pair_left", [P, 2, CAND])
        top_s = sb("top_s", [P, 2, TOPK])
        top_u = sb("top_u", [P, 2, TOPK], U32)
        top_f = sb("top_f", [P, 2 * TOPK])
        is_cand = sb("is_cand", [P, 2 * TOPK, CAND])
        top_d = sb("top_d", [P, 2, TOPK])
        top_e = sb("top_e", [P, 2, TOPK])
        top_sum = sb("top_sum", [P, 2])
        top_rsum = sb("top_rsum", [P, 2])

        rows = sb("rows", [P, SLOTS, TOPK, 2 * D])
        diag = sb("diag", [P, 2, TOPK, P])
        kT_sb = sb("kT_sb", [P, 2, P])
        v_sb = sb("v_sb", [P, 2, D])
        at_sm = sb("at_sm", [P, 2, P])
        at_negmax = sb("at_negmax", [P, 2])
        at_sum = sb("at_sum", [P, 2])
        at_rsum = sb("at_rsum", [P, 2])
        at_p = sb("at_p", [P, 2, P])
        at_pn = sb("at_pn", [P, 2, P])
        at_pT_sb = sb("at_pT_sb", [P, 2, P])
        at_oT_sb = sb("at_oT_sb", [P, 2, P])

        x2 = sb("x2", [P, D])
        x3 = sb("x3", [P, D])
        mh_sb = sb("mh_sb", [P, D + 1])
        deg_c = sb("deg_c", [P, 3])
        upd_b = sb("upd_b", [P, D])
        node_sum = sb("node_sum", [P, D])
        wts = sb("wts", [P, G])
        wts_tmp = sb("wts_tmp", [P, G])
        own_w = sb("own_w", [P, 1])
        rank_gt = sb("rank_gt", [P, 1])
        rank_eq = sb("rank_eq", [P, 1])
        rank = sb("rank", [P, 1])
        scale_w = sb("scale_w", [P, 1])
        hid = sb("hid", [P, HC, P])
        hid_a = sb("hid_a", [P, HC, P])
        hid_e = sb("hid_e", [P, HC, P])
        hid_g = sb("hid_g", [P, HC, P])
        y_sb = sb("y_sb", [P, D])

        ps_sim = [ctx.enter_context(nc.psum_tensor(f"ps_sim{i}", [P, 4, P], F32)) for i in range(2)]
        ps_k = ctx.enter_context(nc.psum_tensor("ps_k", [P, P], F32))
        ps_v = ctx.enter_context(nc.psum_tensor("ps_v", [P, D], F32))
        ps_at = ctx.enter_context(nc.psum_tensor("ps_at", [P, 3, P], F32))
        ps_acc = ctx.enter_context(nc.psum_tensor("ps_acc", [P, D], F32))
        ps_f = ctx.enter_context(nc.psum_tensor("ps_f", [P, 4, P], F32))
        ps_b = ctx.enter_context(nc.psum_tensor("ps_b", [P, 4, P], F32))

        consts_loaded = sem("consts_loaded")
        consts_made = sem("consts_made")
        consts_spread = sem("consts_spread")
        x_loaded = sems("x_loaded", 2)
        adj_loaded = sems("adj_loaded", 2)
        var_ready = sems("var_ready", 4)
        rstd_ready = sems("rstd_ready", 4)
        xn_ready = sems("xn_ready", 4)
        xnT_psum = sems("xnT_psum", 4)
        xnT_ready = sems("xnT_ready", 4)
        gat_h = sem("gat_h")
        gat_hT_sb = sem("gat_hT_sb")
        gat_h_sb = sem("gat_h_sb")
        gat_e = sem("gat_e")
        gat_e_sb = sem("gat_e_sb")
        gat_max = sem("gat_max")
        gat_exp = sem("gat_exp")
        gat_pT = sem("gat_pT")
        gat_pT_done = sem("gat_pT_done")
        gat_o = sem("gat_o")
        q_psum = sem("q_psum")
        q_copied = sem("q_copied")
        sim_ready = sem("sim_ready")
        sim_used = sem("sim_used")
        top_ready = sem("top_ready")
        top_exp = sem("top_exp")
        choice_ready = sem("choice_ready")
        rows_landed = sems("rows_landed", SLOTS)
        pool_go = sem("pool_go")
        vec_go = sem("vec_go")
        diag_ready = sem("diag_ready")
        k_done = sem("k_done")
        v_done = sem("v_done")
        k_copied = sem("k_copied")
        v_copied = sem("v_copied")
        at_s = sem("at_s")
        at_max = sem("at_max")
        at_exp = sem("at_exp")
        at_norm = sem("at_norm")
        at_pT = sem("at_pT")
        at_pT_done = sem("at_pT_done")
        at_oT = sem("at_oT")
        at_oT_done = sem("at_oT_done")
        mem_out = sem("mem_out")
        x2_ready = sem("x2_ready")
        msg_h = sem("msg_h")
        msg_h_sb = sem("msg_h_sb")
        msg_sum = sem("msg_sum")
        x3_ready = sem("x3_ready")
        ffn_in = sem("ffn_in")
        gelu_arg = sem("gelu_arg")
        gelu_exp = sem("gelu_exp")
        gelu_ready = sem("gelu_ready")
        ffn_out = sem("ffn_out")
        out_ready = sem("out_ready")
        stored = sems("stored", 2)
        vec_steps = sem("vec_steps")
        act_steps = sem("act_steps")

        CONSTS = [
            (gat_w_sb[:, :], gat_wT), (a_cols[:, :], gat_a), (wq_pk_sb[:, :], wq_pk),
            (keys_sb[0:DK, :, 0, :], keysT[0:DK]), (keys_sb[DK:P, :, 1, :], keysT[DK:P]), (wq_sb[:, :], wq), (wo_sb[:, :, :], wo.rearrange("(h d) n -> d h n", d=D)),
            (w_msg_sb[:, :], w_msg), (w_upd_sb[:, :], w_upd), (bias_sb[:, :], bias.partition_broadcast(P)),
            (wr_col[:, :], wr), (br_sb[:, :], br.partition_broadcast(P)), (w1_sb[:, :], w1),
            (b1_sb[:, :], b1), (w2_sb[:, :, :], w2.rearrange("(c p) n -> p c n", p=P)),
            (b2_sb[:, :], b2.partition_broadcast(P)),
        ]
        POOL_CONSTS = 12
        SPREAD = 9

        def heads_before(t):
            return t.n * H

        block = ctx.enter_context(nc.Block())

        @block.sync
        def _(sp):
            def load(t):
                sp.dma_start(x_in[:, t.p, :], x[bass.ds(t.n * P, P), :]).then_inc(x_loaded[t.p], 16)
                sp.dma_start(adj_in[:, t.p, :], adj[bass.ds(t.n * P, P), :]).then_inc(adj_loaded[t.p], 16)

            def step(t, ahead):
                if ahead:
                    sp.wait_ge(var_ready[1], t.n + 1)
                    load(Tile(t.i + 1, t.p))
                sp.wait_ge(out_ready, t.n + 1)
                sp.dma_start(out[bass.ds(t.n * P, P), :], out_sb[:, t.p, :]).then_inc(stored[t.p], 16)

            sp.sem_inc(stored[0], 16)
            sp.sem_inc(stored[1], 16)
            load(Tile(0, 0))
            sp.wait_ge(consts_made, 1)
            for dst, src in CONSTS:
                sp.dma_start(dst, src).then_inc(consts_loaded, 16)
            load(Tile(0, 1))
            with sp.Fori(0, TILES // 2 - 1) as i:
                step(Tile(i, 0), True)
                step(Tile(i, 1), True)
            step(Tile(TILES // 2 - 1, 0), False)
            step(Tile(TILES // 2 - 1, 1), False)
            for p in range(2):
                sp.wait_ge(stored[p], 16 * (TILES // 2 + 1))

        @block.gpsimd
        def _(pool):
            pool.memset(keys_sb[:, :, :, :], 0.0).then_inc(consts_made, 1)
            pool.memset(ident[:, :], 0.0).then_inc(consts_made, 1)
            pool.memset(causal[:, :], 0.0).then_inc(consts_made, 1)
            pool.memset(before[:, :], 1.0).then_inc(consts_made, 1)
            pool.memset(neg_edge[:, :], NEG_EDGE).then_inc(consts_made, 1)
            pool.memset(adj_f[:, :, :], 0.0).then_inc(consts_made, 1)
            pool.memset(gat_p[:, :], 0.0).then_inc(consts_made, 1)
            pool.memset(mh_sb[:, D:D + 1], 1.0).then_inc(consts_made, 1)
            pool.iota(cand_pos_i[:, :], [[1, CAND]], base=0, channel_multiplier=0).then_inc(consts_made, 1)
            pool.wait_ge(consts_made, 9)
            pool.affine_select(out=ident[:, :], in_=ident[:, :], compare_op=ALU.not_equal, fill=1.0, base=0,
                               pattern=[[-1, P]], channel_multiplier=1).then_inc(consts_made, 1)
            pool.affine_select(out=before[:, :], in_=before[:, :], compare_op=ALU.is_gt, fill=0.0, base=0,
                               pattern=[[-1, P]], channel_multiplier=1).then_inc(consts_made, 1)
            pool.affine_select(out=causal[:, :], in_=causal[:, :], compare_op=ALU.is_ge, fill=NEG_CAUSAL, base=0,
                               pattern=[[-1, P]], channel_multiplier=1).then_inc(consts_made, 1)

            def gathers(t):
                for h in range(H):
                    slot = h % SLOTS
                    pool.wait_ge(choice_ready, t.n * 4 + h // 2 + 1)
                    pool.wait_ge(v_done, heads_before(t) + h + 1)
                    pool.sem_inc(pool_go, 1)
                    for j in range(TOPK):
                        pool.indirect_dma_start(
                            out=rows[:, slot, j, :], out_offset=None, in_=table,
                            in_offset=bass.IndirectOffsetOnAxis(ap=row_idx[:, t.p, h, j:j + 1], axis=0),
                        ).then_inc(rows_landed[slot], 16)

            with pool.Fori(0, TILES // 2) as i:
                gathers(Tile(i, 0))
                gathers(Tile(i, 1))

        @block.vector
        def _(dve):
            own = Steps(dve, vec_steps)
            mark, then, settle = own.mark, own.then, own.settle
            V = nc.vector

            def norm_stats(t, j, src):
                then(V.bn_stats(ln_stats[:, j, :], src))
                then(V.bn_aggr(ln_mv[:, j, :], ln_stats[:, j, :]))
                V.tensor_scalar(ln_ve[:, j:j + 1], ln_mv[:, j, 1:2], EPS, None, ALU.add).then_inc(var_ready[j], 1)

            def norm_apply(t, j, src):
                ve, r0, c, r = (b[:, j:j + 1] for b in (ln_ve, ln_r0, ln_c, ln_r))
                dve.wait_ge(rstd_ready[j], t.n + 1)
                then(V.scalar_tensor_tensor(c, r0, r0, ve, ALU.mult, ALU.mult))
                then(V.tensor_scalar(c, c, -0.5, 1.5, ALU.mult, ALU.add))
                then(V.tensor_tensor(r, r0, c, ALU.mult))
                V.tensor_scalar(xn[:, j, :], src, ln_mv[:, j, 0:1], r, ALU.subtract, ALU.mult).then_inc(xn_ready[j], 1)

            def graph_attention(t):
                dve.wait_ge(x_loaded[t.p], (t.i + 1) * 16)
                norm_stats(t, 0, x_in[:, t.p, :])
                dve.wait_ge(adj_loaded[t.p], (t.i + 1) * 16)
                for g in range(2):
                    r = slice(g * G, (g + 1) * G)
                    mark(V.tensor_copy(adj_f[r, t.p, r], adj_in[r, t.p, :]))
                mark(V.tensor_scalar(no_edge[:, :], adj_in[:, t.p, :], 0.0, None, ALU.is_equal))
                norm_apply(t, 0, x_in[:, t.p, :])
                dve.wait_ge(gat_e_sb, t.n + 1)
                then(V.scalar_tensor_tensor(edge[:, :], edge_raw[:, :], 0.2, edge_raw[:, :], ALU.mult, ALU.max))
                then(V.copy_predicated(edge[:, :], no_edge[:, :], neg_edge[:, :]))
                V.tensor_reduce(gat_negmax[:, :], edge[:, :], AX.X, ALU.max, negate=True).then_inc(gat_max, 1)
                dve.wait_ge(gat_exp, t.n + 1)
                mark(V.reciprocal(gat_rsum[:, :], gat_sum[:, :]))
                dve.wait_ge(gat_o, t.n + 1)
                settle()
                then(V.scalar_tensor_tensor(x1[:, t.p, :], ps_f[:, 1, :], gat_rsum[:, :], x_in[:, t.p, :],
                                            ALU.mult, ALU.add))
                norm_stats(t, 1, x1[:, t.p, :])
                norm_apply(t, 1, x1[:, t.p, :])

            def keys_first(t, q):
                dve.wait_ge(sim_ready, t.n * 4 + q + 1)
                dve.sem_inc(vec_go, 1)
                for c in range(4):
                    mark(V.max(best[:, c % 2, c // 2, 0:8], ps_sim[q % 2][:, c, :]))
                settle()

            def keys_rest(t, q):
                sims = ps_sim[q % 2]
                for c in range(4):
                    mark(V.match_replace(left[:, c, :], best[:, c % 2, c // 2, 0:8], sims[:, c, :], NEG_TAKEN))
                for c in range(4):
                    ins = V.max_index(best_u[:, c % 2, c // 2, 0:8], best[:, c % 2, c // 2, 0:8], sims[:, c, :])
                    if c < 3:
                        mark(ins)
                    else:
                        ins.then_inc(sim_used, 1)
                settle()
                for c in range(4):
                    mark(V.max(best[:, c % 2, c // 2, 8:16], left[:, c, :]))
                settle()
                for c in range(4):
                    mark(V.max_index(best_u[:, c % 2, c // 2, 8:16], best[:, c % 2, c // 2, 8:16], left[:, c, :]))

            def pair_scores(t, q):
                settle()
                mark(V.tensor_copy(best_f[:, :, 0, :], best_u[:, :, 0, :]))
                for e in range(2):
                    mark(V.tensor_scalar(best_f[:, e, 1, :], best_u[:, e, 1, :], float(NKEY),
                                         float((2 * q + e) * NKEY * NKEY), ALU.mult, ALU.add))
                for vals, dst in ((best, pair_s), (best_f, pair_i)):
                    if vals is best_f:
                        settle()
                    at = 0
                    for i0, ni, nj in BLOCKS:
                        a = vals[:, :, 0, i0:i0 + ni].unsqueeze(3).to_broadcast([P, 2, ni, nj])
                        b = vals[:, :, 1, 0:nj].unsqueeze(2).to_broadcast([P, 2, ni, nj])
                        o = dst[:, :, at:at + ni * nj].rearrange("p e (i j) -> p e i j", i=ni)
                        mark(V.tensor_tensor(o, a, b, ALU.add))
                        at += ni * nj

            def pairs_best(t, q):
                settle()
                for e in range(2):
                    mark(V.max(top_s[:, e, 0:8], pair_s[:, e, :]))
                settle()
                for e in range(2):
                    mark(V.match_replace(pair_left[:, e, :], top_s[:, e, 0:8], pair_s[:, e, :], NEG_TAKEN))
                for e in range(2):
                    mark(V.max_index(top_u[:, e, 0:8], top_s[:, e, 0:8], pair_s[:, e, :]))
                settle()
                for e in range(2):
                    mark(V.max(top_s[:, e, 8:16], pair_left[:, e, :]))
                settle()
                for e in range(2):
                    mark(V.max_index(top_u[:, e, 8:16], top_s[:, e, 8:16], pair_left[:, e, :]))
                V.tensor_tensor(top_d[:, :, :], top_s[:, :, :], top_s[:, :, 0:1].to_broadcast([P, 2, TOPK]),
                                ALU.subtract).then_inc(top_ready, 1)
                settle()
                then(V.tensor_copy(top_f[:, :], top_u[:, :, :].rearrange("p e k -> p (e k)")))
                then(V.tensor_tensor(is_cand[:, :, :], cand_pos[:, :].unsqueeze(1).to_broadcast([P, 2 * TOPK, CAND]),
                                     top_f[:, :].unsqueeze(2).to_broadcast([P, 2 * TOPK, CAND]), ALU.is_equal))
                own_i = is_cand[:, :, :].rearrange("p (e k) c -> p e k c", e=2)
                then(V.tensor_tensor(own_i, own_i, pair_i[:, :, :].unsqueeze(2).to_broadcast([P, 2, TOPK, CAND]),
                                     ALU.mult))
                hs = slice(2 * q, 2 * q + 2)
                with nc.allow_low_precision(reason="sums of one whole number below 2**17 and zeros"):
                    mark(V.tensor_reduce(row_idx[:, t.p, hs, :].rearrange("p e k -> p (e k)"), is_cand[:, :, :],
                                         AX.X, ALU.add))
                dve.wait_ge(top_exp, t.n * 4 + q + 1)
                then(V.tensor_reduce(top_sum[:, :], top_e[:, :, :], AX.X, ALU.add))
                then(V.reciprocal(top_rsum[:, :], top_sum[:, :]))
                V.tensor_tensor(row_w[:, t.p, hs, :], top_e[:, :, :],
                                top_rsum[:, :].unsqueeze(2).to_broadcast([P, 2, TOPK]),
                                ALU.mult).then_inc(choice_ready, 1)

            def scores_max(t, h):
                b = h % 2
                dve.wait_ge(at_s, heads_before(t) + h + 1)
                then(V.tensor_tensor(at_sm[:, b, :], ps_at[:, 0, :], causal[:, :], ALU.add))
                V.tensor_reduce(at_negmax[:, b:b + 1], at_sm[:, b, :], AX.X, ALU.max, negate=True).then_inc(at_max, 1)

            def scores_norm(t, h):
                b = h % 2
                dve.wait_ge(at_exp, heads_before(t) + h + 1)
                then(V.reciprocal(at_rsum[:, b:b + 1], at_sum[:, b:b + 1]))
                V.tensor_scalar(at_pn[:, b, :], at_p[:, b, :], at_rsum[:, b:b + 1], None, ALU.mult).then_inc(at_norm, 1)

            def message_passing(t):
                dve.wait_ge(mem_out, t.n + 1)
                then(V.tensor_tensor(x2[:, :], ps_acc[:, :], x1[:, t.p, :], ALU.add))
                norm_stats(t, 2, x2[:, :])
                norm_apply(t, 2, x2[:, :])
                dve.wait_ge(msg_sum, t.n + 1)
                deg = ps_at[:, 1, 0:1]
                mark(V.tensor_scalar(deg_c[:, 0:1], deg, 1.0, None, ALU.max))
                mark(V.tensor_scalar(deg_c[:, 1:2], deg, 0.0, None, ALU.is_gt))
                mark(V.tensor_tensor(upd_b[:, :], ps_b[:, 2, :], bias_sb[:, :], ALU.add))
                settle()
                then(V.reciprocal(deg_c[:, 2:3], deg_c[:, 0:1]))
                then(V.tensor_tensor(deg_c[:, 0:1], deg_c[:, 1:2], deg_c[:, 2:3], ALU.mult))
                then(V.scalar_tensor_tensor(node_sum[:, :], ps_at[:, 0, :], deg_c[:, 0:1], upd_b[:, :],
                                            ALU.mult, ALU.add))
                then(V.scalar_tensor_tensor(x3[:, :], node_sum[:, :], 0.0, x2[:, :], ALU.max, ALU.add))

            def heavy_ffn(t):
                norm_stats(t, 3, x3[:, :])
                norm_apply(t, 3, x3[:, :])
                dve.wait_ge(ffn_in, t.n + 1)
                then(V.tensor_tensor(hid[:, :, :], ps_sim[0][:, :, :],
                                     b1_sb[:, :].unsqueeze(2).to_broadcast([P, HC, P]), ALU.add))
                then(V.tensor_tensor(hid_a[:, :, :], hid[:, :, :], hid[:, :, :], ALU.mult))
                then(V.tensor_scalar(hid_a[:, :, :], hid_a[:, :, :], GELU_A, 1.0, ALU.mult, ALU.add))
                then(V.tensor_tensor(hid_a[:, :, :], hid_a[:, :, :], hid[:, :, :], ALU.mult))
                V.tensor_scalar(hid_a[:, :, :], hid_a[:, :, :], -50.0, -GELU_C, ALU.max, ALU.mult).then_inc(gelu_arg, 1)
                for g in range(2):
                    r = slice(g * G, (g + 1) * G)
                    mark(V.tensor_scalar(wts[r, :], ps_b[r, 1, r], br_sb[r, :], None, ALU.add))
                settle()
                then(V.scalar_tensor_tensor(wts_tmp[:, :], wts[:, :], 1.0, ident_g[:, :], ALU.mult, ALU.mult,
                                            accum_out=own_w[:, :]))
                then(V.tensor_scalar(wts_tmp[:, :], wts[:, :], own_w[:, :], None, ALU.is_gt, ALU.add,
                                     accum_out=rank_gt[:, :]))
                then(V.scalar_tensor_tensor(wts_tmp[:, :], wts[:, :], own_w[:, :], before_g[:, :], ALU.is_equal,
                                            ALU.mult, accum_out=rank_eq[:, :]))
                then(V.tensor_tensor(rank[:, :], rank_gt[:, :], rank_eq[:, :], ALU.add))
                mark(V.scalar_tensor_tensor(scale_w[:, :], rank[:, :], KEPT - 0.5, own_w[:, :], ALU.is_lt, ALU.mult))
                dve.wait_ge(gelu_exp, t.n + 1)
                then(V.tensor_scalar(hid_e[:, :, :], hid_e[:, :, :], 1.0, None, ALU.add))
                then(V.reciprocal(hid_e[:, :, :], hid_e[:, :, :]))
                V.tensor_tensor(hid_g[:, :, :], hid[:, :, :], hid_e[:, :, :], ALU.mult).then_inc(gelu_ready, 1)
                dve.wait_ge(ffn_out, t.n + 1)
                then(V.tensor_tensor(y_sb[:, :], ps_sim[1][:, 0, :], b2_sb[:, :], ALU.add))
                then(V.scalar_tensor_tensor(y_sb[:, :], y_sb[:, :], scale_w[:, :], xn[:, 3, :], ALU.mult, ALU.add))
                dve.wait_ge(stored[t.p], (t.i + 1) * 16)
                V.tensor_tensor(out_sb[:, t.p, :], y_sb[:, :], x3[:, :], ALU.add).then_inc(out_ready, 1)

            def step(t, front):
                nt = t.next()
                if front:
                    graph_attention(nt)
                for m in range(H + 1):
                    q = m // 2
                    if m >= 1:
                        scores_max(t, m - 1)
                    if front and m < H and m % 2 == 0:
                        keys_first(nt, q)
                    if m >= 1:
                        scores_norm(t, m - 1)
                    if front and m < H:
                        if m % 2 == 0:
                            keys_rest(nt, q)
                            pair_scores(nt, q)
                        else:
                            pairs_best(nt, q)
                message_passing(t)
                heavy_ffn(t)
                own.restart()

            dve.wait_ge(consts_made, POOL_CONSTS)
            dve.wait_ge(consts_loaded, 16 * len(CONSTS))
            V.tensor_copy(a_left[:, :], a_cols[:, 0:1].to_broadcast([P, P])).then_inc(consts_spread, 1)
            V.tensor_copy(a_right[:, :], a_cols[:, 1:2].to_broadcast([P, P])).then_inc(consts_spread, 1)
            V.tensor_copy(wr_sb[:, :], wr_col[:, 0:1].to_broadcast([P, P])).then_inc(consts_spread, 1)
            V.tensor_copy(cand_pos[:, :], cand_pos_i[:, :]).then_inc(consts_spread, 1)
            for g in range(2):
                r = slice(g * G, (g + 1) * G)
                V.tensor_copy(ident_g[r, :], ident[r, r]).then_inc(consts_spread, 1)
                V.tensor_copy(before_g[r, :], before[r, r]).then_inc(consts_spread, 1)
            V.memset(causal[G:P, 0:G], NEG_CAUSAL).then_inc(consts_spread, 1)
            dve.wait_ge(consts_spread, SPREAD)
            dve.sem_inc(sim_used, 2)
            first = Tile(0, 0)
            graph_attention(first)
            for q in range(4):
                keys_first(first, q)
                keys_rest(first, q)
                pair_scores(first, q)
                pairs_best(first, q)
            own.restart()
            with dve.Fori(0, TILES // 2 - 1) as i:
                step(Tile(i, 0), True)
                step(Tile(i, 1), True)
            step(Tile(TILES // 2 - 1, 0), True)
            step(Tile(TILES // 2 - 1, 1), False)

        @block.scalar
        def _(act):
            own = Steps(act, act_steps)
            A = nc.scalar

            def rstd(t, j):
                act.wait_ge(var_ready[j], t.n + 1)
                own.then(A.activation(ln_log[:, j:j + 1], ln_ve[:, j:j + 1], ACT.Ln))
                A.activation(ln_r0[:, j:j + 1], ln_log[:, j:j + 1], ACT.Exp, scale=-0.5).then_inc(rstd_ready[j], 1)
                act.wait_ge(xnT_psum[j], t.n + 1)
                A.copy(xnT[:, j, :], (ps_f if j < 2 else ps_b)[:, 0, :]).then_inc(xnT_ready[j], 1)

            def graph_attention(t):
                rstd(t, 0)
                act.wait_ge(gat_h, t.n + 1)
                A.copy(ghT_sb[:, :], ps_f[:, 2, :]).then_inc(gat_hT_sb, 1)
                A.copy(gh_sb[:, :], ps_f[:, 1, :]).then_inc(gat_h_sb, 1)
                act.wait_ge(gat_e, t.n + 1)
                for g in range(2):
                    r = slice(g * G, (g + 1) * G)
                    ins = A.copy(edge_raw[r, :], ps_f[r, 3, r])
                ins.then_inc(gat_e_sb, 1)
                act.wait_ge(gat_max, t.n + 1)
                for g in range(2):
                    r = slice(g * G, (g + 1) * G)
                    ins = A.activation(gat_p[r, r], edge[r, :], ACT.Exp, bias=gat_negmax[r, :],
                                       accum_out=gat_sum[r, :])
                ins.then_inc(gat_exp, 1)
                act.wait_ge(gat_pT, t.n + 1)
                A.copy(gat_pT_sb[:, :], ps_f[:, 0, :]).then_inc(gat_pT_done, 1)
                rstd(t, 1)

            def queries(t):
                for part in range(4):
                    act.wait_ge(q_psum, t.n * 4 + part + 1)
                    if part < 2:
                        dst, s = qT[:, t.p, 4 * part:4 * part + 4, :], float(D) ** -0.5
                    else:
                        dst, s = qpT[:, 4 * (part - 2):4 * (part - 2) + 4, :], 1.0
                    A.mul(dst, ps_sim[part % 2][:, :, :], s).then_inc(q_copied, 1)

            def top_exps(t, q):
                act.wait_ge(top_ready, t.n * 4 + q + 1)
                A.activation(top_e[:, :, :], top_d[:, :, :], ACT.Exp).then_inc(top_exp, 1)

            def diagonals(t, h):
                b = h % 2
                act.wait_ge(choice_ready, t.n * 4 + h // 2 + 1)
                act.wait_ge(v_done, heads_before(t) + h + 1 - 2 + SLOTS)
                for j in range(TOPK):
                    ins = A.activation(diag[:, b, j, :], ident[:, :], ACT.Copy, scale=row_w[:, t.p, h, j:j + 1])
                ins.then_inc(diag_ready, 1)

            def copy_k(t, h):
                act.wait_ge(k_done, heads_before(t) + h + 1)
                A.copy(kT_sb[:, h % 2, :], ps_k[:, :]).then_inc(k_copied, 1)

            def copy_v(t, h):
                act.wait_ge(v_done, heads_before(t) + h + 1 + SLOTS)
                A.copy(v_sb[:, h % 2, :], ps_v[:, :]).then_inc(v_copied, 1)

            def scores_exp(t, h):
                b = h % 2
                act.wait_ge(at_max, heads_before(t) + h + 1)
                A.activation(at_p[:, b, :], at_sm[:, b, :], ACT.Exp, bias=at_negmax[:, b:b + 1],
                             accum_out=at_sum[:, b:b + 1]).then_inc(at_exp, 1)

            def copy_pT(t, h):
                act.wait_ge(at_pT, heads_before(t) + h + 1)
                A.copy(at_pT_sb[:, h % 2, :], ps_at[:, 1, :]).then_inc(at_pT_done, 1)

            def copy_oT(t, h):
                act.wait_ge(at_oT, heads_before(t) + h + 1)
                A.copy(at_oT_sb[:, h % 2, :], ps_at[:, 2, :]).then_inc(at_oT_done, 1)

            def step(t, front):
                nt = t.next()
                if front:
                    graph_attention(nt)
                    queries(nt)
                diagonals(t, 0)
                for m in range(H + 1):
                    if m >= 1:
                        scores_exp(t, m - 1)
                    if m + 1 < H:
                        diagonals(t, m + 1)
                    if m >= 1:
                        copy_pT(t, m - 1)
                    if m < H:
                        copy_k(t, m)
                        copy_v(t, m)
                    if m >= 1:
                        copy_oT(t, m - 1)
                    if front and m < H and m % 2 == 1:
                        top_exps(nt, m // 2)
                rstd(t, 2)
                act.wait_ge(msg_h, t.n + 1)
                A.copy(mh_sb[:, 0:D], ps_b[:, 1, :]).then_inc(msg_h_sb, 1)
                rstd(t, 3)
                act.wait_ge(gelu_arg, t.n + 1)
                A.activation(hid_e[:, :, :], hid_a[:, :, :], ACT.Exp).then_inc(gelu_exp, 1)
                own.restart()

            A.preload_act_table_set("natural_log_exp_and_others")
            act.wait_ge(consts_made, POOL_CONSTS)
            first = Tile(0, 0)
            graph_attention(first)
            queries(first)
            for q in range(4):
                top_exps(first, q)
            own.restart()
            with act.Fori(0, TILES // 2 - 1) as i:
                step(Tile(i, 0), True)
                step(Tile(i, 1), True)
            step(Tile(TILES // 2 - 1, 0), True)
            step(Tile(TILES // 2 - 1, 1), False)

        @block.tensor
        def _(pe):
            T = nc.tensor

            def mm(out, lhsT, rhs, start=True, stop=True):
                return T.matmul(out, lhsT, rhs, start=start, stop=stop)

            def transposed(t, j):
                pe.wait_ge(xn_ready[j], t.n + 1)
                T.transpose((ps_f if j < 2 else ps_b)[:, 0, :], xn[:, j, :], ident[:, :]).then_inc(xnT_psum[j], 1)
                pe.wait_ge(xnT_ready[j], t.n + 1)

            def graph_attention(t):
                transposed(t, 0)
                mm(ps_f[:, 1, :], xnT[:, 0, :], gat_w_sb[:, :])
                mm(ps_f[:, 2, :], gat_w_sb[:, :], xnT[:, 0, :]).then_inc(gat_h, 1)
                pe.wait_ge(gat_hT_sb, t.n + 1)
                pe.wait_ge(gat_h_sb, t.n + 1)
                mm(ps_f[:, 3, :], ghT_sb[:, :], a_left[:, :], stop=False)
                mm(ps_f[:, 3, :], a_right[:, :], ghT_sb[:, :], start=False).then_inc(gat_e, 1)
                pe.wait_ge(gat_exp, t.n + 1)
                T.transpose(ps_f[:, 0, :], gat_p[:, :], ident[:, :]).then_inc(gat_pT, 1)
                pe.wait_ge(gat_pT_done, t.n + 1)
                mm(ps_f[:, 1, :], gat_pT_sb[:, :], gh_sb[:, :]).then_inc(gat_o, 1)
                transposed(t, 1)

            def queries(t):
                pe.wait_ge(sim_used, t.n * 4 + 2)
                for part in range(4):
                    if part >= 2:
                        pe.wait_ge(q_copied, t.n * 4 + part - 1)
                    w = wq_sb if part < 2 else wq_pk_sb
                    for c in range(4):
                        n = 4 * (part % 2) + c
                        ins = mm(ps_sim[part % 2][:, c, :], w[:, n * P:(n + 1) * P], xnT[:, 1, :])
                    ins.then_inc(q_psum, 1)
                pe.wait_ge(q_copied, t.n * 4 + 4)

            def similarities(t, q):
                pe.wait_ge(sim_used, t.n * 4 + q + 1)
                for side in range(2):
                    chunk = 4 * side + q
                    ins = mm(ps_sim[q % 2][:, 2 * side:2 * side + 2, :], qpT[:, chunk, :], keys_sb[:, chunk, :, :])
                ins.then_inc(sim_ready, 1)

            def rows_to_k(t, h):
                slot, b = h % SLOTS, h % 2
                pe.wait_ge(diag_ready, heads_before(t) + h + 1)
                pe.wait_ge(rows_landed[slot], (t.n * (H // SLOTS) + h // SLOTS + 1) * (16 * TOPK))
                for j in range(TOPK):
                    ins = mm(ps_k[:, :], rows[:, slot, j, 0:D], diag[:, b, j, :], start=j == 0, stop=j == TOPK - 1)
                ins.then_inc(k_done, 1)

            def rows_to_v(t, h):
                slot, b = h % SLOTS, h % 2
                if h >= 1:
                    pe.wait_ge(v_copied, heads_before(t) + h)
                for j in range(TOPK):
                    ins = mm(ps_v[:, :], diag[:, b, j, :], rows[:, slot, j, D:2 * D], start=j == 0, stop=j == TOPK - 1)
                ins.then_inc(v_done, 1)

            def scores(t, h):
                pe.wait_ge(k_copied, heads_before(t) + h + 1)
                mm(ps_at[:, 0, :], qT[:, t.p, h, :], kT_sb[:, h % 2, :]).then_inc(at_s, 1)

            def turn_p(t, h):
                pe.wait_ge(at_norm, heads_before(t) + h + 1)
                T.transpose(ps_at[:, 1, :], at_pn[:, h % 2, :], ident[:, :]).then_inc(at_pT, 1)

            def attend(t, h):
                pe.wait_ge(v_copied, heads_before(t) + h + 1)
                pe.wait_ge(at_pT_done, heads_before(t) + h + 1)
                mm(ps_at[:, 2, :], v_sb[:, h % 2, :], at_pT_sb[:, h % 2, :]).then_inc(at_oT, 1)

            def project(t, h):
                pe.wait_ge(at_oT_done, heads_before(t) + h + 1)
                ins = mm(ps_acc[:, :], at_oT_sb[:, h % 2, :], wo_sb[:, h, :], start=h == 0, stop=h == H - 1)
                if h == H - 1:
                    ins.then_inc(mem_out, 1)

            def step(t, front):
                nt = t.next()
                if front:
                    graph_attention(nt)
                    queries(nt)
                for m in range(H + 1):
                    if m >= 2:
                        project(t, m - 2)
                    if m >= 1:
                        scores(t, m - 1)
                    if front and m < H and m % 2 == 0:
                        similarities(nt, m // 2)
                    if m < H:
                        rows_to_k(t, m)
                    if m >= 1:
                        turn_p(t, m - 1)
                    if m < H:
                        rows_to_v(t, m)
                    if m >= 1:
                        attend(t, m - 1)
                project(t, H - 1)
                transposed(t, 2)
                mm(ps_b[:, 2, :], xnT[:, 2, :], w_upd_sb[:, :])
                mm(ps_b[:, 1, :], xnT[:, 2, :], w_msg_sb[:, :]).then_inc(msg_h, 1)
                pe.wait_ge(msg_h_sb, t.n + 1)
                mm(ps_at[:, 0, :], adj_f[:, t.p, :], mh_sb[:, 0:D])
                mm(ps_at[:, 1, 0:1], adj_f[:, t.p, :], mh_sb[:, D:D + 1]).then_inc(msg_sum, 1)
                transposed(t, 3)
                mm(ps_b[:, 1, :], wr_sb[:, :], xnT[:, 3, :])
                if front:
                    pe.wait_ge(sim_used, nt.n * 4 + 6)
                for c in range(HC):
                    ins = mm(ps_sim[0][:, c, :], w1_sb[:, c * P:(c + 1) * P], xnT[:, 3, :])
                ins.then_inc(ffn_in, 1)
                pe.wait_ge(gelu_ready, t.n + 1)
                for c in range(HC):
                    ins = mm(ps_sim[1][:, 0, :], hid_g[:, c, :], w2_sb[:, c, :], start=c == 0, stop=c == HC - 1)
                ins.then_inc(ffn_out, 1)

            pe.sem_inc(v_done, SLOTS)
            pe.wait_ge(consts_made, POOL_CONSTS)
            pe.wait_ge(consts_loaded, 16 * len(CONSTS))
            pe.wait_ge(consts_spread, SPREAD)
            first = Tile(0, 0)
            graph_attention(first)
            queries(first)
            for q in range(4):
                similarities(first, q)
            with pe.Fori(0, TILES // 2 - 1) as i:
                step(Tile(i, 0), True)
                step(Tile(i, 1), True)
            step(Tile(TILES // 2 - 1, 0), True)
            step(Tile(TILES // 2 - 1, 1), False)


def layout(x, adj, L0_gnn_W, L0_gnn_a, L0_ffn_Wq_pk, L0_ffn_pk_keys, L0_ffn_Wq, L0_ffn_keys_table,
           L0_ffn_values_table, L0_ffn_Wo, L1_gnn_W_msg, L1_gnn_W_upd, L1_gnn_bias, L1_ffn_wr, L1_ffn_br,
           L1_ffn_w1, L1_ffn_b1, L1_ffn_w2, L1_ffn_b2):
    c = np.ascontiguousarray
    keys = np.asarray(L0_ffn_pk_keys)
    keys = keys.transpose(2, 3, 0, 1).reshape(4, 2, DK, 2, NKEY)
    keys = keys.transpose(1, 2, 3, 0, 4).reshape(P, H, NKEY)
    return {
        "x": c(np.asarray(x).reshape(-1, D)), "adj": c(np.asarray(adj).reshape(-1, G)),
        "gat_wT": c(np.asarray(L0_gnn_W).T), "gat_a": c(np.asarray(L0_gnn_a).reshape(2, D).T),
        "wq_pk": c(L0_ffn_Wq_pk), "keysT": c(keys), "wq": c(L0_ffn_Wq),
        "table": np.concatenate([np.asarray(L0_ffn_keys_table), np.asarray(L0_ffn_values_table)], axis=1),
        "wo": c(L0_ffn_Wo), "w_msg": c(L1_gnn_W_msg), "w_upd": c(L1_gnn_W_upd), "bias": c(L1_gnn_bias),
        "wr": c(L1_ffn_wr), "br": c(L1_ffn_br), "w1": c(L1_ffn_w1),
        "b1": c(np.asarray(L1_ffn_b1).reshape(HC, P).T), "w2": c(L1_ffn_w2), "b2": c(L1_ffn_b2),
    }


def kernel(**inputs):
    import concourse.bacc as _bacc
    from concourse.bass_utils import run_bass_kernel_spmd as _run

    inputs = dict(inputs)
    inputs.pop("L1_ffn_attention_mask")
    shape = inputs["x"].shape
    nc = _bacc.Bacc("TRN2", target_bir_lowering=False, num_devices=1)
    arrays = {f"in_{k}_dram": a for k, a in layout(**inputs).items()}
    args = [nc.dram_tensor(k, a.shape, mybir.dt.from_np(a.dtype), kind="ExternalInput").ap()
            for k, a in arrays.items()]
    out = nc.dram_tensor("out_dram", (shape[0] * shape[1], shape[2]), F32, kind="ExternalOutput").ap()
    build(nc, *args, out)
    r = _run(nc, [arrays], core_ids=[0])
    return r.results[0]["out_dram"].reshape(shape)
```

```python
from contextlib import ExitStack

import numpy as np
import concourse.bass as bass
from concourse import mybir

ALU = mybir.AluOpType
ACT = mybir.ActivationFunctionType
AX = mybir.AxisListType
F32 = mybir.dt.float32
U32 = mybir.dt.uint32
I32 = mybir.dt.int32

P = 128
G = 64
D = 128
H = 8
TOPK = 16
NKEY = 128
DK = 64
HID = 512
HC = HID // P
KEPT = 31
SLOTS = 4
ROW_GROUPS = ((0, 5), (5, 11), (11, TOPK))
HALF = HC // 2
EPS = 1e-5
NEG_EDGE = -1.0e9
NEG_CAUSAL = -1.0e30
NEG_TAKEN = -3.0e38
GELU_C = 1.5957691216057308
GELU_A = 0.044715

BLOCKS = ((0, 1, 16), (1, 1, 8), (2, 2, 5), (4, 4, 3), (8, 8, 1))
CAND = sum(ni * nj for _, ni, nj in BLOCKS)


class Tile:

    def __init__(self, i, p):
        self.i, self.p, self.n = i, p, i * 2 + p

    def next(self):
        return Tile(self.i, 1) if self.p == 0 else Tile(self.i + 1, 0)


class Steps:

    def __init__(self, eng, sem):
        self.eng, self.sem, self.count = eng, sem, 0

    def mark(self, ins):
        self.count += 1
        ins.then_inc(self.sem, 1)

    def settle(self):
        self.eng.wait_ge(self.sem, self.count)

    def then(self, ins):
        self.mark(ins)
        self.settle()

    def restart(self):
        self.settle()
        self.eng.sem_clear(self.sem)
        self.count = 0


def build(nc, x, adj, gat_wT, gat_a, wq_pk, keysT, wq, table, wo, w_msg, w_upd, bias, wr, br, w1, b1, w2, b2, out):
    TILES = x.shape[0] // P
    ctx = ExitStack()
    with ctx:
        def sb(name, shape, dt=F32):
            return ctx.enter_context(nc.sbuf_tensor(name, shape, dt))

        def sem(name):
            return ctx.enter_context(nc.semaphore(name))

        def sems(name, n):
            return [sem(f"{name}{i}") for i in range(n)]

        ident = sb("ident", [P, P])
        ident_g = sb("ident_g", [P, G])
        before_g = sb("before_g", [P, G])
        before = sb("before", [P, P])
        causal = sb("causal", [P, P])
        neg_edge = sb("neg_edge", [P, G])
        cand_pos_i = sb("cand_pos_i", [P, CAND], I32)
        cand_pos = sb("cand_pos", [P, CAND])
        gat_w_sb = sb("gat_w_sb", [P, D])
        a_cols = sb("a_cols", [P, 2])
        a_left = sb("a_left", [P, P])
        a_right = sb("a_right", [P, P])
        wq_pk_sb = sb("wq_pk_sb", [P, 2 * H * DK])
        keys_sb = sb("keys_sb", [P, H, 2, NKEY])
        wq_sb = sb("wq_sb", [P, H * D])
        wo_sb = sb("wo_sb", [P, H, D])
        w_msg_sb = sb("w_msg_sb", [P, D])
        w_upd_sb = sb("w_upd_sb", [P, D])
        bias_sb = sb("bias_sb", [P, D])
        wr_col = sb("wr_col", [P, 1])
        wr_sb = sb("wr_sb", [P, P])
        br_sb = sb("br_sb", [P, 1])
        w1_sb = sb("w1_sb", [P, HID])
        b1_sb = sb("b1_sb", [P, HC])
        w2_sb = sb("w2_sb", [P, HC, D])
        b2_sb = sb("b2_sb", [P, D])

        x_in = sb("x_in", [P, 2, D])
        adj_in = sb("adj_in", [P, 2, G], I32)
        adj_f = sb("adj_f", [P, 2, P])
        x1 = sb("x1", [P, 2, D])
        qT = sb("qT", [P, 2, H, P])
        row_idx = sb("row_idx", [P, 2, H, TOPK], U32)
        row_w = sb("row_w", [P, 2, H, TOPK])
        out_sb = sb("out_sb", [P, 2, D])

        ln_stats = sb("ln_stats", [P, 4, 6])
        ln_mv = sb("ln_mv", [P, 4, 2])
        ln_ve = sb("ln_ve", [P, 4])
        ln_log = sb("ln_log", [P, 4])
        ln_r0 = sb("ln_r0", [P, 4])
        ln_c = sb("ln_c", [P, 4])
        ln_r = sb("ln_r", [P, 4])
        xn = sb("xn", [P, 4, D])
        xnT = sb("xnT", [P, 4, P])

        gh_sb = sb("gh_sb", [P, D])
        ghT_sb = sb("ghT_sb", [P, P])
        no_edge = sb("no_edge", [P, G], I32)
        edge_raw = sb("edge_raw", [P, G])
        edge = sb("edge", [P, G])
        gat_negmax = sb("gat_negmax", [P, 1])
        gat_sum = sb("gat_sum", [P, 1])
        gat_rsum = sb("gat_rsum", [P, 1])
        gat_p = sb("gat_p", [P, P])
        gat_pT_sb = sb("gat_pT_sb", [P, P])

        qpT = sb("qpT", [P, H, P])
        best = sb("best", [P, 2, 2, TOPK])
        best_u = sb("best_u", [P, 2, 2, TOPK], U32)
        best_f = sb("best_f", [P, 2, 2, TOPK])
        left = sb("left", [P, 4, NKEY])
        pair_s = sb("pair_s", [P, 2, CAND])
        pair_i = sb("pair_i", [P, 2, CAND])
        pair_left = sb("pair_left", [P, 2, CAND])
        top_s = sb("top_s", [P, 2, TOPK])
        top_u = sb("top_u", [P, 2, TOPK], U32)
        top_f = sb("top_f", [P, 2 * TOPK])
        is_cand = sb("is_cand", [P, 2 * TOPK, CAND])
        top_d = sb("top_d", [P, 2, TOPK])
        top_e = sb("top_e", [P, 2, TOPK])
        top_sum = sb("top_sum", [P, 2])
        top_rsum = sb("top_rsum", [P, 2])

        rows = sb("rows", [P, SLOTS, TOPK, 2 * D])
        diag = sb("diag", [P, 2, TOPK, P])
        kT_sb = sb("kT_sb", [P, 2, P])
        kv_sb = sb("kv_sb", [P, 2, 2 * D])
        at_sm = sb("at_sm", [P, 2, P])
        at_negmax = sb("at_negmax", [P, 2])
        at_sum = sb("at_sum", [P, 2])
        at_rsum = sb("at_rsum", [P, 2])
        at_p = sb("at_p", [P, 2, P])
        at_pn = sb("at_pn", [P, 2, P])
        at_pT_sb = sb("at_pT_sb", [P, 2, P])
        at_oT_sb = sb("at_oT_sb", [P, 2, P])

        x2 = sb("x2", [P, D])
        x3 = sb("x3", [P, D])
        mh_sb = sb("mh_sb", [P, D + 1])
        deg_c = sb("deg_c", [P, 3])
        upd_b = sb("upd_b", [P, D])
        node_sum = sb("node_sum", [P, D])
        wts = sb("wts", [P, G])
        wts_tmp = sb("wts_tmp", [P, G])
        own_w = sb("own_w", [P, 1])
        rank_gt = sb("rank_gt", [P, 1])
        rank_eq = sb("rank_eq", [P, 1])
        rank = sb("rank", [P, 1])
        scale_w = sb("scale_w", [P, 1])
        hid = sb("hid", [P, HC, P])
        hid_q = sb("hid_q", [P, HC, P])
        hid_a = sb("hid_a", [P, HC, P])
        hid_e = sb("hid_e", [P, HC, P])
        hid_g = sb("hid_g", [P, HC, P])
        y_sb = sb("y_sb", [P, D])

        ps_sim = [ctx.enter_context(nc.psum_tensor(f"ps_sim{i}", [P, 4, P], F32)) for i in range(2)]
        ps_kv = [ctx.enter_context(nc.psum_tensor(f"ps_kv{i}", [P, 2 * D], F32)) for i in range(2)]
        ps_at = ctx.enter_context(nc.psum_tensor("ps_at", [P, 4, P], F32))
        ps_acc = ctx.enter_context(nc.psum_tensor("ps_acc", [P, D], F32))
        ps_f = ctx.enter_context(nc.psum_tensor("ps_f", [P, 4, P], F32))
        ps_b = ctx.enter_context(nc.psum_tensor("ps_b", [P, 4, P], F32))

        gat_consts_loaded = sem("gat_consts_loaded")
        consts_loaded = sem("consts_loaded")
        consts_made = sem("consts_made")
        consts_spread = sem("consts_spread")
        x_loaded = sems("x_loaded", 2)
        adj_loaded = sems("adj_loaded", 2)
        var_ready = sems("var_ready", 4)
        rstd_ready = sems("rstd_ready", 4)
        xn_ready = sems("xn_ready", 4)
        xnT_psum = sems("xnT_psum", 4)
        xnT_ready = sems("xnT_ready", 4)
        gat_h = sem("gat_h")
        gat_hT_sb = sem("gat_hT_sb")
        gat_h_sb = sem("gat_h_sb")
        gat_e = sem("gat_e")
        gat_e_sb = sem("gat_e_sb")
        gat_max = sem("gat_max")
        gat_exp = sem("gat_exp")
        gat_pT = sem("gat_pT")
        gat_pT_done = sem("gat_pT_done")
        gat_o = sem("gat_o")
        q_psum = sem("q_psum")
        q_copied = sem("q_copied")
        sim_ready = sem("sim_ready")
        sim_used = sem("sim_used")
        top_ready = sem("top_ready")
        top_exp = sem("top_exp")
        choice_ready = sem("choice_ready")
        rows_landed = [sems(f"rows_landed{h}_", len(ROW_GROUPS)) for h in range(H)]
        pool_go = sem("pool_go")
        vec_go = sem("vec_go")
        diag_ready = sem("diag_ready")
        kv_done = sem("kv_done")
        kv_copied = sem("kv_copied")
        at_kT = sem("at_kT")
        at_kT_done = sem("at_kT_done")
        at_s = sem("at_s")
        at_max = sem("at_max")
        at_exp = sem("at_exp")
        at_norm = sem("at_norm")
        at_pT = sem("at_pT")
        at_pT_done = sem("at_pT_done")
        at_oT = sem("at_oT")
        at_oT_done = sem("at_oT_done")
        mem_out = sem("mem_out")
        x2_ready = sem("x2_ready")
        msg_h = sem("msg_h")
        msg_h_sb = sem("msg_h_sb")
        msg_sum = sem("msg_sum")
        x3_ready = sem("x3_ready")
        ffn_in = sem("ffn_in")
        hid_ready = sem("hid_ready")
        hid_square = sem("hid_square")
        gelu_arg = sem("gelu_arg")
        gelu_exp = sem("gelu_exp")
        gelu_ready = sem("gelu_ready")
        ffn_out = sem("ffn_out")
        out_ready = sem("out_ready")
        stored = sems("stored", 2)
        vec_steps = sem("vec_steps")
        act_steps = sem("act_steps")

        GAT_CONSTS = [(a_cols[:, :], gat_a), (gat_w_sb[:, :], gat_wT)]
        CONSTS = [
            (wq_pk_sb[:, :], wq_pk), (keys_sb[0:DK, :, 0, :], keysT[0:DK]), (keys_sb[DK:P, :, 1, :], keysT[DK:P]),
            (wq_sb[:, :], wq), (wo_sb[:, :, :], wo.rearrange("(h d) n -> d h n", d=D)),
            (w_msg_sb[:, :], w_msg), (w_upd_sb[:, :], w_upd), (bias_sb[:, :], bias.partition_broadcast(P)),
            (wr_col[:, :], wr), (br_sb[:, :], br.partition_broadcast(P)), (w1_sb[:, :], w1),
            (b1_sb[:, :], b1), (w2_sb[:, :, :], w2.rearrange("(c p) n -> p c n", p=P)),
            (b2_sb[:, :], b2.partition_broadcast(P)),
        ]
        POOL_CONSTS = 12
        SPREAD = 9

        def heads_before(t):
            return t.n * H

        def head_at(t, nt, m):
            if m < H:
                return t, m
            return (nt, m - H) if nt else None

        Q_BANK = (0, 1, 1, 0)

        block = ctx.enter_context(nc.Block())

        @block.sync
        def _(sp):
            def load(t):
                sp.dma_start(x_in[:, t.p, :], x[bass.ds(t.n * P, P), :]).then_inc(x_loaded[t.p], 16)
                sp.dma_start(adj_in[:, t.p, :], adj[bass.ds(t.n * P, P), :]).then_inc(adj_loaded[t.p], 16)

            def step(t, ahead):
                if ahead:
                    sp.wait_ge(var_ready[1], t.n + 1)
                    load(Tile(t.i + 1, t.p))
                sp.wait_ge(out_ready, t.n + 1)
                sp.dma_start(out[bass.ds(t.n * P, P), :], out_sb[:, t.p, :]).then_inc(stored[t.p], 16)

            sp.sem_inc(stored[0], 16)
            sp.sem_inc(stored[1], 16)
            load(Tile(0, 0))
            for dst, src in GAT_CONSTS:
                sp.dma_start(dst, src).then_inc(gat_consts_loaded, 16)
            sp.wait_ge(consts_made, 1)
            for dst, src in CONSTS:
                sp.dma_start(dst, src).then_inc(consts_loaded, 16)
            load(Tile(0, 1))
            with sp.Fori(0, TILES // 2 - 1) as i:
                step(Tile(i, 0), True)
                step(Tile(i, 1), True)
            step(Tile(TILES // 2 - 1, 0), False)
            step(Tile(TILES // 2 - 1, 1), False)
            for p in range(2):
                sp.wait_ge(stored[p], 16 * (TILES // 2 + 1))

        @block.gpsimd
        def _(pool):
            pool.memset(keys_sb[:, :, :, :], 0.0).then_inc(consts_made, 1)
            pool.memset(ident[:, :], 0.0).then_inc(consts_made, 1)
            pool.memset(causal[:, :], 0.0).then_inc(consts_made, 1)
            pool.memset(before[:, :], 1.0).then_inc(consts_made, 1)
            pool.memset(neg_edge[:, :], NEG_EDGE).then_inc(consts_made, 1)
            pool.memset(adj_f[:, :, :], 0.0).then_inc(consts_made, 1)
            pool.memset(gat_p[:, :], 0.0).then_inc(consts_made, 1)
            pool.memset(mh_sb[:, D:D + 1], 1.0).then_inc(consts_made, 1)
            pool.iota(cand_pos_i[:, :], [[1, CAND]], base=0, channel_multiplier=0).then_inc(consts_made, 1)
            pool.wait_ge(consts_made, 9)
            pool.affine_select(out=ident[:, :], in_=ident[:, :], compare_op=ALU.not_equal, fill=1.0, base=0,
                               pattern=[[-1, P]], channel_multiplier=1).then_inc(consts_made, 1)
            pool.affine_select(out=before[:, :], in_=before[:, :], compare_op=ALU.is_gt, fill=0.0, base=0,
                               pattern=[[-1, P]], channel_multiplier=1).then_inc(consts_made, 1)
            pool.affine_select(out=causal[:, :], in_=causal[:, :], compare_op=ALU.is_ge, fill=NEG_CAUSAL, base=0,
                               pattern=[[-1, P]], channel_multiplier=1).then_inc(consts_made, 1)

            def gathers(t):
                for h in range(H):
                    slot = h % SLOTS
                    pool.wait_ge(choice_ready, t.n * 4 + h // 2 + 1)
                    pool.wait_ge(kv_done, heads_before(t) + h + 1)
                    pool.sem_inc(pool_go, 1)
                    for group, (j0, j1) in enumerate(ROW_GROUPS):
                        for j in range(j0, j1):
                            pool.indirect_dma_start(
                                out=rows[:, slot, j, :], out_offset=None, in_=table,
                                in_offset=bass.IndirectOffsetOnAxis(ap=row_idx[:, t.p, h, j:j + 1], axis=0),
                            ).then_inc(rows_landed[h][group], 16)

            with pool.Fori(0, TILES // 2) as i:
                gathers(Tile(i, 0))
                gathers(Tile(i, 1))

        @block.vector
        def _(dve):
            own = Steps(dve, vec_steps)
            mark, then, settle = own.mark, own.then, own.settle
            V = nc.vector

            def norm_stats(t, j, src):
                then(V.bn_stats(ln_stats[:, j, :], src))
                then(V.bn_aggr(ln_mv[:, j, :], ln_stats[:, j, :]))
                V.tensor_scalar(ln_ve[:, j:j + 1], ln_mv[:, j, 1:2], EPS, None, ALU.add).then_inc(var_ready[j], 1)

            def norm_apply(t, j, src):
                ve, r0, c, r = (b[:, j:j + 1] for b in (ln_ve, ln_r0, ln_c, ln_r))
                dve.wait_ge(rstd_ready[j], t.n + 1)
                then(V.scalar_tensor_tensor(c, r0, r0, ve, ALU.mult, ALU.mult))
                then(V.tensor_scalar(c, c, -0.5, 1.5, ALU.mult, ALU.add))
                then(V.tensor_tensor(r, r0, c, ALU.mult))
                V.tensor_scalar(xn[:, j, :], src, ln_mv[:, j, 0:1], r, ALU.subtract, ALU.mult).then_inc(xn_ready[j], 1)

            def g0_stats(t):
                dve.wait_ge(x_loaded[t.p], (t.i + 1) * 16)
                norm_stats(t, 0, x_in[:, t.p, :])

            def g4_edges(t):
                dve.wait_ge(adj_loaded[t.p], (t.i + 1) * 16)
                for g in range(2):
                    r = slice(g * G, (g + 1) * G)
                    mark(V.tensor_copy(adj_f[r, t.p, r], adj_in[r, t.p, :]))
                mark(V.tensor_scalar(no_edge[:, :], adj_in[:, t.p, :], 0.0, None, ALU.is_equal))
                dve.wait_ge(gat_e_sb, t.n + 1)
                then(V.scalar_tensor_tensor(edge[:, :], edge_raw[:, :], 0.2, edge_raw[:, :], ALU.mult, ALU.max))
                then(V.copy_predicated(edge[:, :], no_edge[:, :], neg_edge[:, :]))
                V.tensor_reduce(gat_negmax[:, :], edge[:, :], AX.X, ALU.max, negate=True).then_inc(gat_max, 1)

            def g5_sum(t):
                dve.wait_ge(gat_exp, t.n + 1)
                mark(V.reciprocal(gat_rsum[:, :], gat_sum[:, :]))

            def g6_residual(t):
                dve.wait_ge(gat_o, t.n + 1)
                settle()
                then(V.scalar_tensor_tensor(x1[:, t.p, :], ps_f[:, 1, :], gat_rsum[:, :], x_in[:, t.p, :],
                                            ALU.mult, ALU.add))
                norm_stats(t, 1, x1[:, t.p, :])

            def keys_first(t, q):
                dve.wait_ge(sim_ready, t.n * 4 + q + 1)
                dve.sem_inc(vec_go, 1)
                for c in range(4):
                    mark(V.max(best[:, c % 2, c // 2, 0:8], ps_sim[q % 2][:, c, :]))
                settle()

            def keys_rest(t, q):
                sims = ps_sim[q % 2]
                for c in range(4):
                    mark(V.match_replace(left[:, c, :], best[:, c % 2, c // 2, 0:8], sims[:, c, :], NEG_TAKEN))
                for c in range(4):
                    ins = V.max_index(best_u[:, c % 2, c // 2, 0:8], best[:, c % 2, c // 2, 0:8], sims[:, c, :])
                    if c < 3:
                        mark(ins)
                    else:
                        ins.then_inc(sim_used, 1)
                settle()
                for c in range(4):
                    mark(V.max(best[:, c % 2, c // 2, 8:16], left[:, c, :]))
                settle()
                for c in range(4):
                    mark(V.max_index(best_u[:, c % 2, c // 2, 8:16], best[:, c % 2, c // 2, 8:16], left[:, c, :]))

            def pair_scores(t, q):
                settle()
                mark(V.tensor_copy(best_f[:, :, 0, :], best_u[:, :, 0, :]))
                for e in range(2):
                    mark(V.tensor_scalar(best_f[:, e, 1, :], best_u[:, e, 1, :], float(NKEY),
                                         float((2 * q + e) * NKEY * NKEY), ALU.mult, ALU.add))
                for vals, dst in ((best, pair_s), (best_f, pair_i)):
                    if vals is best_f:
                        settle()
                    at = 0
                    for i0, ni, nj in BLOCKS:
                        a = vals[:, :, 0, i0:i0 + ni].unsqueeze(3).to_broadcast([P, 2, ni, nj])
                        b = vals[:, :, 1, 0:nj].unsqueeze(2).to_broadcast([P, 2, ni, nj])
                        o = dst[:, :, at:at + ni * nj].rearrange("p e (i j) -> p e i j", i=ni)
                        mark(V.tensor_tensor(o, a, b, ALU.add))
                        at += ni * nj

            def pairs_best(t, q):
                settle()
                for e in range(2):
                    mark(V.max(top_s[:, e, 0:8], pair_s[:, e, :]))
                settle()
                for e in range(2):
                    mark(V.match_replace(pair_left[:, e, :], top_s[:, e, 0:8], pair_s[:, e, :], NEG_TAKEN))
                for e in range(2):
                    mark(V.max_index(top_u[:, e, 0:8], top_s[:, e, 0:8], pair_s[:, e, :]))
                settle()
                for e in range(2):
                    mark(V.max(top_s[:, e, 8:16], pair_left[:, e, :]))
                settle()
                for e in range(2):
                    mark(V.max_index(top_u[:, e, 8:16], top_s[:, e, 8:16], pair_left[:, e, :]))
                V.tensor_tensor(top_d[:, :, :], top_s[:, :, :], top_s[:, :, 0:1].to_broadcast([P, 2, TOPK]),
                                ALU.subtract).then_inc(top_ready, 1)
                settle()
                then(V.tensor_copy(top_f[:, :], top_u[:, :, :].rearrange("p e k -> p (e k)")))
                then(V.tensor_tensor(is_cand[:, :, :], cand_pos[:, :].unsqueeze(1).to_broadcast([P, 2 * TOPK, CAND]),
                                     top_f[:, :].unsqueeze(2).to_broadcast([P, 2 * TOPK, CAND]), ALU.is_equal))
                own_i = is_cand[:, :, :].rearrange("p (e k) c -> p e k c", e=2)
                then(V.tensor_tensor(own_i, own_i, pair_i[:, :, :].unsqueeze(2).to_broadcast([P, 2, TOPK, CAND]),
                                     ALU.mult))
                hs = slice(2 * q, 2 * q + 2)
                with nc.allow_low_precision(reason="sums of one whole number below 2**17 and zeros"):
                    mark(V.tensor_reduce(row_idx[:, t.p, hs, :].rearrange("p e k -> p (e k)"), is_cand[:, :, :],
                                         AX.X, ALU.add))
                dve.wait_ge(top_exp, t.n * 4 + q + 1)
                then(V.tensor_reduce(top_sum[:, :], top_e[:, :, :], AX.X, ALU.add))
                then(V.reciprocal(top_rsum[:, :], top_sum[:, :]))
                V.tensor_tensor(row_w[:, t.p, hs, :], top_e[:, :, :],
                                top_rsum[:, :].unsqueeze(2).to_broadcast([P, 2, TOPK]),
                                ALU.mult).then_inc(choice_ready, 1)

            def scores_max(t, h):
                b = h % 2
                dve.wait_ge(at_s, heads_before(t) + h + 1)
                then(V.tensor_tensor(at_sm[:, b, :], ps_at[:, 1, :], causal[:, :], ALU.add))
                V.tensor_reduce(at_negmax[:, b:b + 1], at_sm[:, b, :], AX.X, ALU.max, negate=True).then_inc(at_max, 1)

            def scores_norm(t, h):
                b = h % 2
                dve.wait_ge(at_exp, heads_before(t) + h + 1)
                then(V.reciprocal(at_rsum[:, b:b + 1], at_sum[:, b:b + 1]))
                V.tensor_scalar(at_pn[:, b, :], at_p[:, b, :], at_rsum[:, b:b + 1], None, ALU.mult).then_inc(at_norm, 1)

            def t0_residual(t):
                dve.wait_ge(mem_out, t.n + 1)
                then(V.tensor_tensor(x2[:, :], ps_acc[:, :], x1[:, t.p, :], ALU.add))
                norm_stats(t, 2, x2[:, :])

            def t3_messages(t):
                dve.wait_ge(msg_sum, t.n + 1)
                deg = ps_at[:, 1, 0:1]
                mark(V.tensor_scalar(deg_c[:, 0:1], deg, 1.0, None, ALU.max))
                mark(V.tensor_scalar(deg_c[:, 1:2], deg, 0.0, None, ALU.is_gt))
                mark(V.tensor_tensor(upd_b[:, :], ps_b[:, 2, :], bias_sb[:, :], ALU.add))
                settle()
                then(V.reciprocal(deg_c[:, 2:3], deg_c[:, 0:1]))
                then(V.tensor_tensor(deg_c[:, 0:1], deg_c[:, 1:2], deg_c[:, 2:3], ALU.mult))
                then(V.scalar_tensor_tensor(node_sum[:, :], ps_at[:, 0, :], deg_c[:, 0:1], upd_b[:, :],
                                            ALU.mult, ALU.add))
                then(V.scalar_tensor_tensor(x3[:, :], node_sum[:, :], 0.0, x2[:, :], ALU.max, ALU.add))
                norm_stats(t, 3, x3[:, :])

            def t5_hidden(t):
                dve.wait_ge(ffn_in, t.n + 1)
                for half in range(2):
                    cs = slice(half * HALF, (half + 1) * HALF)
                    V.tensor_tensor(hid[:, cs, :], ps_sim[0][:, cs, :],
                                    b1_sb[:, cs].unsqueeze(2).to_broadcast([P, HALF, P]), ALU.add).then_inc(hid_ready, 1)
                for g in range(2):
                    r = slice(g * G, (g + 1) * G)
                    mark(V.tensor_scalar(wts[r, :], ps_b[r, 1, r], br_sb[r, :], None, ALU.add))

            def t6_gelu_arg(t):
                for half in range(2):
                    cs = slice(half * HALF, (half + 1) * HALF)
                    dve.wait_ge(hid_square, t.n * 2 + half + 1)
                    then(V.tensor_tensor(hid_a[:, cs, :], hid_q[:, cs, :], hid[:, cs, :], ALU.mult))
                    V.tensor_scalar(hid_a[:, cs, :], hid_a[:, cs, :], -50.0, -GELU_C, ALU.max,
                                    ALU.mult).then_inc(gelu_arg, 1)
                then(V.scalar_tensor_tensor(wts_tmp[:, :], wts[:, :], 1.0, ident_g[:, :], ALU.mult, ALU.mult,
                                            accum_out=own_w[:, :]))
                then(V.tensor_scalar(wts_tmp[:, :], wts[:, :], own_w[:, :], None, ALU.is_gt, ALU.add,
                                     accum_out=rank_gt[:, :]))
                then(V.scalar_tensor_tensor(wts_tmp[:, :], wts[:, :], own_w[:, :], before_g[:, :], ALU.is_equal,
                                            ALU.mult, accum_out=rank_eq[:, :]))
                then(V.tensor_tensor(rank[:, :], rank_gt[:, :], rank_eq[:, :], ALU.add))
                mark(V.scalar_tensor_tensor(scale_w[:, :], rank[:, :], KEPT - 0.5, own_w[:, :], ALU.is_lt, ALU.mult))

            def t7_gelu(t):
                for half in range(2):
                    cs = slice(half * HALF, (half + 1) * HALF)
                    dve.wait_ge(gelu_exp, t.n * 2 + half + 1)
                    then(V.reciprocal(hid_e[:, cs, :], hid_e[:, cs, :]))
                    V.tensor_tensor(hid_g[:, cs, :], hid[:, cs, :], hid_e[:, cs, :], ALU.mult).then_inc(gelu_ready, 1)

            def t8_out(t):
                dve.wait_ge(ffn_out, t.n + 1)
                then(V.tensor_tensor(y_sb[:, :], ps_acc[:, :], b2_sb[:, :], ALU.add))
                then(V.scalar_tensor_tensor(y_sb[:, :], y_sb[:, :], scale_w[:, :], xn[:, 3, :], ALU.mult, ALU.add))
                dve.wait_ge(stored[t.p], (t.i + 1) * 16)
                V.tensor_tensor(out_sb[:, t.p, :], y_sb[:, :], x3[:, :], ALU.add).then_inc(out_ready, 1)

            def turns(t, nn):
                if t: t0_residual(t)
                if nn: g0_stats(nn)
                if t: norm_apply(t, 2, x2[:, :])
                if nn: norm_apply(nn, 0, x_in[:, nn.p, :])
                if t: t3_messages(t)
                if nn: g4_edges(nn)
                if t: norm_apply(t, 3, x3[:, :])
                if nn: g5_sum(nn)
                if t: t5_hidden(t)
                if nn: g6_residual(nn)
                if t: t6_gelu_arg(t)
                if nn: norm_apply(nn, 1, x1[:, nn.p, :])
                if t: t7_gelu(t)
                if t: t8_out(t)
                own.restart()

            def step(t, choose, start):
                nt = t.next() if choose else None
                for m in range(1, H + 1):
                    scores_max(t, m - 1)
                    if nt and m % 2 == 1:
                        keys_first(nt, m // 2)
                    scores_norm(t, m - 1)
                    if nt and m % 2 == 1:
                        keys_rest(nt, m // 2)
                        pair_scores(nt, m // 2)
                    elif nt:
                        pairs_best(nt, m // 2 - 1)
                turns(t, nt.next() if start else None)

            dve.wait_ge(consts_made, POOL_CONSTS)
            dve.wait_ge(gat_consts_loaded, 16 * len(GAT_CONSTS))
            V.tensor_copy(a_left[:, :], a_cols[:, 0:1].to_broadcast([P, P])).then_inc(consts_spread, 1)
            V.tensor_copy(a_right[:, :], a_cols[:, 1:2].to_broadcast([P, P])).then_inc(consts_spread, 1)
            V.tensor_copy(cand_pos[:, :], cand_pos_i[:, :]).then_inc(consts_spread, 1)
            for g in range(2):
                r = slice(g * G, (g + 1) * G)
                V.tensor_copy(ident_g[r, :], ident[r, r]).then_inc(consts_spread, 1)
                V.tensor_copy(before_g[r, :], before[r, r]).then_inc(consts_spread, 1)
            V.memset(causal[G:P, 0:G], NEG_CAUSAL).then_inc(consts_spread, 1)
            dve.sem_inc(sim_used, 2)
            first = Tile(0, 0)
            turns(None, first)
            dve.wait_ge(consts_loaded, 16 * len(CONSTS))
            V.tensor_copy(wr_sb[:, :], wr_col[:, 0:1].to_broadcast([P, P])).then_inc(consts_spread, 1)
            dve.wait_ge(consts_spread, SPREAD)
            for q in range(4):
                keys_first(first, q)
                keys_rest(first, q)
                pair_scores(first, q)
                pairs_best(first, q)
            own.restart()
            turns(None, first.next())
            with dve.Fori(0, TILES // 2 - 1) as i:
                step(Tile(i, 0), True, True)
                step(Tile(i, 1), True, True)
            step(Tile(TILES // 2 - 1, 0), True, False)
            step(Tile(TILES // 2 - 1, 1), False, False)

        @block.scalar
        def _(act):
            own = Steps(act, act_steps)
            A = nc.scalar

            def rstd(t, j):
                act.wait_ge(var_ready[j], t.n + 1)
                own.then(A.activation(ln_log[:, j:j + 1], ln_ve[:, j:j + 1], ACT.Ln))
                A.activation(ln_r0[:, j:j + 1], ln_log[:, j:j + 1], ACT.Exp, scale=-0.5).then_inc(rstd_ready[j], 1)

            def copy_xnT(t, j):
                act.wait_ge(xnT_psum[j], t.n + 1)
                A.copy(xnT[:, j, :], (ps_f if j < 2 else ps_b)[:, 0, :]).then_inc(xnT_ready[j], 1)

            def g2_copies(t):
                act.wait_ge(gat_h, t.n + 1)
                A.copy(ghT_sb[:, :], ps_f[:, 2, :]).then_inc(gat_hT_sb, 1)
                A.copy(gh_sb[:, :], ps_f[:, 1, :]).then_inc(gat_h_sb, 1)

            def g3_copy(t):
                act.wait_ge(gat_e, t.n + 1)
                for g in range(2):
                    r = slice(g * G, (g + 1) * G)
                    ins = A.copy(edge_raw[r, :], ps_f[r, 3, r])
                ins.then_inc(gat_e_sb, 1)

            def g4_exp(t):
                act.wait_ge(gat_max, t.n + 1)
                for g in range(2):
                    r = slice(g * G, (g + 1) * G)
                    ins = A.activation(gat_p[r, r], edge[r, :], ACT.Exp, bias=gat_negmax[r, :],
                                       accum_out=gat_sum[r, :])
                ins.then_inc(gat_exp, 1)

            def g5_copy(t):
                act.wait_ge(gat_pT, t.n + 1)
                A.copy(gat_pT_sb[:, :], ps_f[:, 0, :]).then_inc(gat_pT_done, 1)

            def g8_queries(t, parts):
                for part in parts:
                    act.wait_ge(q_psum, t.n * 4 + part + 1)
                    if part < 2:
                        dst, s = qpT[:, 4 * part:4 * part + 4, :], 1.0
                    else:
                        dst, s = qT[:, t.p, 4 * (part - 2):4 * (part - 2) + 4, :], float(D) ** -0.5
                    A.mul(dst, ps_sim[Q_BANK[part]][:, :, :], s).then_inc(q_copied, 1)

            def t2_copy(t):
                act.wait_ge(msg_h, t.n + 1)
                A.copy(mh_sb[:, 0:D], ps_b[:, 1, :]).then_inc(msg_h_sb, 1)

            def t5_square(t, half):
                act.wait_ge(hid_ready, t.n * 2 + half + 1)
                cs = slice(half * HALF, (half + 1) * HALF)
                own.then(A.activation(hid_q[:, cs, :], hid[:, cs, :], ACT.Square))
                A.activation(hid_q[:, cs, :], hid_q[:, cs, :], ACT.Copy, bias=1.0, scale=GELU_A).then_inc(hid_square, 1)

            def t6_exp(t, half):
                act.wait_ge(gelu_arg, t.n * 2 + half + 1)
                cs = slice(half * HALF, (half + 1) * HALF)
                own.then(A.activation(hid_e[:, cs, :], hid_a[:, cs, :], ACT.Exp))
                A.activation(hid_e[:, cs, :], hid_e[:, cs, :], ACT.Copy, bias=1.0).then_inc(gelu_exp, 1)

            def turns(t, nn, queries=(0, 1, 2, 3)):
                if t: rstd(t, 2)
                if nn: rstd(nn, 0)
                if t: copy_xnT(t, 2)
                if nn: copy_xnT(nn, 0)
                if t: t2_copy(t)
                if nn: g2_copies(nn)
                if nn: g3_copy(nn)
                if t: rstd(t, 3)
                if nn: g4_exp(nn)
                if t: copy_xnT(t, 3)
                if nn: g5_copy(nn)
                if t:
                    t5_square(t, 0)
                    t5_square(t, 1)
                if nn: rstd(nn, 1)
                if t:
                    t6_exp(t, 0)
                    t6_exp(t, 1)
                if nn: copy_xnT(nn, 1)
                if nn: g8_queries(nn, queries)
                own.restart()

            def top_exps(t, q):
                act.wait_ge(top_ready, t.n * 4 + q + 1)
                A.activation(top_e[:, :, :], top_d[:, :, :], ACT.Exp).then_inc(top_exp, 1)

            def diagonals(t, h, js):
                b = h % 2
                if js[0] == 0:
                    act.wait_ge(choice_ready, t.n * 4 + h // 2 + 1)
                    act.wait_ge(kv_done, heads_before(t) + h + 1 - 2 + SLOTS)
                for j in js:
                    ins = A.activation(diag[:, b, j, :], ident[:, :], ACT.Copy, scale=row_w[:, t.p, h, j:j + 1])
                if js[-1] == TOPK - 1:
                    ins.then_inc(diag_ready, 1)

            def copy_kv(t, h):
                act.wait_ge(kv_done, heads_before(t) + h + 1 + SLOTS)
                A.copy(kv_sb[:, h % 2, :], ps_kv[h % 2][:, :]).then_inc(kv_copied, 1)

            def copy_kT(t, h):
                act.wait_ge(at_kT, heads_before(t) + h + 1)
                A.copy(kT_sb[:, h % 2, :], ps_at[:, 0, :]).then_inc(at_kT_done, 1)

            def scores_exp(t, h):
                b = h % 2
                act.wait_ge(at_max, heads_before(t) + h + 1)
                A.activation(at_p[:, b, :], at_sm[:, b, :], ACT.Exp, bias=at_negmax[:, b:b + 1],
                             accum_out=at_sum[:, b:b + 1]).then_inc(at_exp, 1)

            def copy_pT(t, h):
                act.wait_ge(at_pT, heads_before(t) + h + 1)
                A.copy(at_pT_sb[:, h % 2, :], ps_at[:, 2, :]).then_inc(at_pT_done, 1)

            def copy_oT(t, h):
                act.wait_ge(at_oT, heads_before(t) + h + 1)
                A.copy(at_oT_sb[:, h % 2, :], ps_at[:, 3, :]).then_inc(at_oT_done, 1)

            def step(t, choose, start):
                nt = t.next() if choose else None
                for m in range(1, H + 1):
                    now, ahead = head_at(t, nt, m), head_at(t, nt, m + 1)
                    copy_kT(t, m - 1)
                    if ahead:
                        diagonals(*ahead, range(0, 5))
                    scores_exp(t, m - 1)
                    if ahead:
                        diagonals(*ahead, range(5, 10))
                    copy_pT(t, m - 1)
                    if ahead:
                        diagonals(*ahead, range(10, TOPK))
                    copy_oT(t, m - 1)
                    if now:
                        copy_kv(*now)
                    if nt and m % 2 == 0:
                        top_exps(nt, m // 2 - 1)
                turns(t, nt.next() if start else None)

            A.preload_act_table_set("natural_log_exp_and_others")
            act.wait_ge(consts_made, POOL_CONSTS)
            first = Tile(0, 0)
            turns(None, first, queries=(0, 1))
            g8_queries(first, (2, 3))
            for q in range(4):
                top_exps(first, q)
            diagonals(first, 0, range(TOPK))
            diagonals(first, 1, range(TOPK))
            copy_kv(first, 0)
            turns(None, first.next())
            with act.Fori(0, TILES // 2 - 1) as i:
                step(Tile(i, 0), True, True)
                step(Tile(i, 1), True, True)
            step(Tile(TILES // 2 - 1, 0), True, False)
            step(Tile(TILES // 2 - 1, 1), False, False)

        @block.tensor
        def _(pe):
            T = nc.tensor

            def mm(out, lhsT, rhs, start=True, stop=True):
                return T.matmul(out, lhsT, rhs, start=start, stop=stop)

            def turn_xn(t, j):
                pe.wait_ge(xn_ready[j], t.n + 1)
                T.transpose((ps_f if j < 2 else ps_b)[:, 0, :], xn[:, j, :], ident[:, :]).then_inc(xnT_psum[j], 1)

            def g2_project(t):
                pe.wait_ge(xnT_ready[0], t.n + 1)
                mm(ps_f[:, 1, :], xnT[:, 0, :], gat_w_sb[:, :])
                mm(ps_f[:, 2, :], gat_w_sb[:, :], xnT[:, 0, :]).then_inc(gat_h, 1)

            def g3_scores(t):
                pe.wait_ge(gat_hT_sb, t.n + 1)
                pe.wait_ge(gat_h_sb, t.n + 1)
                mm(ps_f[:, 3, :], ghT_sb[:, :], a_left[:, :], stop=False)
                mm(ps_f[:, 3, :], a_right[:, :], ghT_sb[:, :], start=False).then_inc(gat_e, 1)

            def g5_turn(t):
                pe.wait_ge(gat_exp, t.n + 1)
                T.transpose(ps_f[:, 0, :], gat_p[:, :], ident[:, :]).then_inc(gat_pT, 1)

            def g6_attend(t):
                pe.wait_ge(gat_pT_done, t.n + 1)
                mm(ps_f[:, 1, :], gat_pT_sb[:, :], gh_sb[:, :]).then_inc(gat_o, 1)

            def g8_queries(t, parts):
                pe.wait_ge(xnT_ready[1], t.n + 1)
                for part in parts:
                    if part == 2:
                        pe.wait_ge(q_copied, t.n * 4 + 2)
                    w = wq_pk_sb if part < 2 else wq_sb
                    for c in range(4):
                        n = 4 * (part % 2) + c
                        ins = mm(ps_sim[Q_BANK[part]][:, c, :], w[:, n * P:(n + 1) * P], xnT[:, 1, :])
                    ins.then_inc(q_psum, 1)

            def g8_read_out(t, parts):
                pe.wait_ge(q_copied, t.n * 4 + parts)

            def t2_messages(t):
                pe.wait_ge(xnT_ready[2], t.n + 1)
                mm(ps_b[:, 2, :], xnT[:, 2, :], w_upd_sb[:, :])
                mm(ps_b[:, 1, :], xnT[:, 2, :], w_msg_sb[:, :]).then_inc(msg_h, 1)

            def t3_sums(t):
                pe.wait_ge(msg_h_sb, t.n + 1)
                mm(ps_at[:, 0, :], adj_f[:, t.p, :], mh_sb[:, 0:D])
                mm(ps_at[:, 1, 0:1], adj_f[:, t.p, :], mh_sb[:, D:D + 1]).then_inc(msg_sum, 1)

            def t5_hidden(t):
                pe.wait_ge(xnT_ready[3], t.n + 1)
                mm(ps_b[:, 1, :], wr_sb[:, :], xnT[:, 3, :])
                for c in range(HC):
                    ins = mm(ps_sim[0][:, c, :], w1_sb[:, c * P:(c + 1) * P], xnT[:, 3, :])
                ins.then_inc(ffn_in, 1)

            def t7_out(t):
                for c in range(HC):
                    if c % HALF == 0:
                        pe.wait_ge(gelu_ready, t.n * 2 + c // HALF + 1)
                    ins = mm(ps_acc[:, :], hid_g[:, c, :], w2_sb[:, c, :], start=c == 0, stop=c == HC - 1)
                ins.then_inc(ffn_out, 1)

            def turns(t, nn, queries=(0, 1, 2, 3)):
                if t: turn_xn(t, 2)
                if nn: turn_xn(nn, 0)
                if t: t2_messages(t)
                if nn: g2_project(nn)
                if t: t3_sums(t)
                if nn: g3_scores(nn)
                if t: turn_xn(t, 3)
                if nn: g5_turn(nn)
                if nn: g6_attend(nn)
                if t: t5_hidden(t)
                if nn: turn_xn(nn, 1)
                if nn and not t: pe.wait_ge(consts_loaded, 16 * len(CONSTS))
                if t: t7_out(t)
                if nn:
                    g8_queries(nn, queries)
                    g8_read_out(nn, len(queries))

            def similarities(t, q):
                pe.wait_ge(sim_used, t.n * 4 + q + 1)
                for side in range(2):
                    chunk = 4 * side + q
                    ins = mm(ps_sim[q % 2][:, 2 * side:2 * side + 2, :], qpT[:, chunk, :], keys_sb[:, chunk, :, :])
                ins.then_inc(sim_ready, 1)

            def weigh_rows(t, h, group):
                slot, b = h % SLOTS, h % 2
                j0, j1 = ROW_GROUPS[group]
                if group == 0:
                    pe.wait_ge(diag_ready, heads_before(t) + h + 1)
                pe.wait_ge(rows_landed[h][group], (t.n + 1) * (16 * (j1 - j0)))
                for j in range(j0, j1):
                    ins = mm(ps_kv[b][:, :], diag[:, b, j, :], rows[:, slot, j, :], start=j == 0, stop=j == TOPK - 1)
                if j1 == TOPK:
                    ins.then_inc(kv_done, 1)

            def turn_k(t, h):
                pe.wait_ge(kv_copied, heads_before(t) + h + 1)
                T.transpose(ps_at[:, 0, :], kv_sb[:, h % 2, 0:D], ident[:, :]).then_inc(at_kT, 1)

            def scores(t, h):
                pe.wait_ge(at_kT_done, heads_before(t) + h + 1)
                mm(ps_at[:, 1, :], qT[:, t.p, h, :], kT_sb[:, h % 2, :]).then_inc(at_s, 1)

            def turn_p(t, h):
                pe.wait_ge(at_norm, heads_before(t) + h + 1)
                T.transpose(ps_at[:, 2, :], at_pn[:, h % 2, :], ident[:, :]).then_inc(at_pT, 1)

            def attend(t, h):
                pe.wait_ge(at_pT_done, heads_before(t) + h + 1)
                mm(ps_at[:, 3, :], kv_sb[:, h % 2, D:2 * D], at_pT_sb[:, h % 2, :]).then_inc(at_oT, 1)

            def project(t, h):
                pe.wait_ge(at_oT_done, heads_before(t) + h + 1)
                ins = mm(ps_acc[:, :], at_oT_sb[:, h % 2, :], wo_sb[:, h, :], start=h == 0, stop=h == H - 1)
                if h == H - 1:
                    ins.then_inc(mem_out, 1)

            def step(t, choose, start):
                nt = t.next() if choose else None
                for m in range(1, H + 1):
                    now = head_at(t, nt, m)
                    if m >= 2:
                        project(t, m - 2)
                    if nt and m % 2 == 1:
                        similarities(nt, m // 2)
                    turn_k(t, m - 1)
                    if now:
                        weigh_rows(*now, 0)
                    scores(t, m - 1)
                    if now:
                        weigh_rows(*now, 1)
                    turn_p(t, m - 1)
                    if now:
                        weigh_rows(*now, 2)
                    attend(t, m - 1)
                project(t, H - 1)
                turns(t, nt.next() if start else None)

            pe.sem_inc(kv_done, SLOTS)
            pe.wait_ge(consts_made, POOL_CONSTS)
            pe.wait_ge(gat_consts_loaded, 16 * len(GAT_CONSTS))
            pe.wait_ge(consts_spread, 2)
            first = Tile(0, 0)
            turns(None, first, queries=(0, 1))
            similarities(first, 0)
            g8_queries(first, (2,))
            pe.wait_ge(sim_used, 3)
            g8_queries(first, (3,))
            g8_read_out(first, 4)
            pe.wait_ge(consts_spread, SPREAD)
            for q in range(1, 4):
                similarities(first, q)
            for group in range(len(ROW_GROUPS)):
                weigh_rows(first, 0, group)
            turns(None, first.next())
            with pe.Fori(0, TILES // 2 - 1) as i:
                step(Tile(i, 0), True, True)
                step(Tile(i, 1), True, True)
            step(Tile(TILES // 2 - 1, 0), True, False)
            step(Tile(TILES // 2 - 1, 1), False, False)


def layout(x, adj, L0_gnn_W, L0_gnn_a, L0_ffn_Wq_pk, L0_ffn_pk_keys, L0_ffn_Wq, L0_ffn_keys_table,
           L0_ffn_values_table, L0_ffn_Wo, L1_gnn_W_msg, L1_gnn_W_upd, L1_gnn_bias, L1_ffn_wr, L1_ffn_br,
           L1_ffn_w1, L1_ffn_b1, L1_ffn_w2, L1_ffn_b2):
    c = np.ascontiguousarray
    keys = np.asarray(L0_ffn_pk_keys)
    keys = keys.transpose(2, 3, 0, 1).reshape(4, 2, DK, 2, NKEY)
    keys = keys.transpose(1, 2, 3, 0, 4).reshape(P, H, NKEY)
    return {
        "x": c(np.asarray(x).reshape(-1, D)), "adj": c(np.asarray(adj).reshape(-1, G)),
        "gat_wT": c(np.asarray(L0_gnn_W).T), "gat_a": c(np.asarray(L0_gnn_a).reshape(2, D).T),
        "wq_pk": c(L0_ffn_Wq_pk), "keysT": c(keys), "wq": c(L0_ffn_Wq),
        "table": np.concatenate([np.asarray(L0_ffn_keys_table), np.asarray(L0_ffn_values_table)], axis=1),
        "wo": c(L0_ffn_Wo), "w_msg": c(L1_gnn_W_msg), "w_upd": c(L1_gnn_W_upd), "bias": c(L1_gnn_bias),
        "wr": c(L1_ffn_wr), "br": c(L1_ffn_br), "w1": c(L1_ffn_w1),
        "b1": c(np.asarray(L1_ffn_b1).reshape(HC, P).T), "w2": c(L1_ffn_w2), "b2": c(L1_ffn_b2),
    }


def kernel(**inputs):
    import concourse.bacc as _bacc
    from concourse.bass_utils import run_bass_kernel_spmd as _run

    inputs = dict(inputs)
    inputs.pop("L1_ffn_attention_mask")
    shape = inputs["x"].shape
    nc = _bacc.Bacc("TRN2", target_bir_lowering=False, num_devices=1)
    arrays = {f"in_{k}_dram": a for k, a in layout(**inputs).items()}
    args = [nc.dram_tensor(k, a.shape, mybir.dt.from_np(a.dtype), kind="ExternalInput").ap()
            for k, a in arrays.items()]
    out = nc.dram_tensor("out_dram", (shape[0] * shape[1], shape[2]), F32, kind="ExternalOutput").ap()
    build(nc, *args, out)
    r = _run(nc, [arrays], core_ids=[0])
    return r.results[0]["out_dram"].reshape(shape)
```
